# Optimizing a Trainium2 kernel written in Bass

```python
import numpy as np
import jax
import jax.numpy as jnp

def _softmax(x, axis=-1):
    return jax.nn.softmax(x, axis=axis)

def _gelu(x):
    return jax.nn.gelu(x, approximate=True)

def _silu(x):
    return jax.nn.silu(x)

def _sigmoid(x):
    return jax.nn.sigmoid(x)

def _layernorm(x, axis=-1, eps=1e-05):
    m = jnp.mean(x, axis=axis, keepdims=True)
    v = jnp.var(x, axis=axis, keepdims=True)
    return (x - m) / jnp.sqrt(v + eps)

def _scatter_add(tgt, idx, src, axis=0):
    return tgt.at[idx].add(src)

def _segment_sum(src, seg, n):
    return jax.ops.segment_sum(src, seg, n)
kernel_name = 'mk_adaln_ffn_d1_seqx_r2_9873a9'

def setup_inputs(seed: int=0):
    np.random.seed(seed)
    _w = jnp.asarray

    def _rec_inputs():
        import jax
        import jax.numpy as jnp
        _rk = jax.random.key(seed)
        x = -0.000125 + 0.9999 * jax.random.normal(jax.random.fold_in(_rk, 1), (8, 512, 2048), jnp.float32)
        _lenS = 512 - jax.random.randint(jax.random.fold_in(_rk, 7), (8,), 0, max(1, 512 // 4) + 1, jnp.int32)
        _lenS2 = 512 - jax.random.randint(jax.random.fold_in(_rk, 8), (8,), 0, max(1, 512 // 4) + 1, jnp.int32)
        itok_B_3_7 = jax.random.randint(jax.random.fold_in(_rk, 11), (8,), 3, 8, jnp.int32)
        return (x, itok_B_3_7)
    x, itok_B_3_7 = _rec_inputs()

    def _L0_cond_setup():
        import jax, jax.numpy as jnp
        import numpy as np
        RANK = 16
        ALPHA = 16.0
        SCALING = ALPHA / RANK
        N_ADAPTERS = 8
        IN_F = 2048
        OUT_F = 2048
        BATCH = 4
        SEQ = 1024
        key = jax.random.key(seed)
        kx, ka, kb, ki = jax.random.split(key, 4)
        x = jax.random.normal(kx, (BATCH, SEQ, IN_F), dtype=jnp.float32)
        A = jax.random.normal(ka, (N_ADAPTERS, OUT_F, RANK), dtype=jnp.float32) * 0.02
        B = jax.random.normal(kb, (N_ADAPTERS, RANK, IN_F), dtype=jnp.float32) * 0.02
        adapter_ids = jax.random.randint(ki, (BATCH,), 0, N_ADAPTERS, dtype=jnp.int32)
        return {'x': x, 'A': A, 'B': B, 'adapter_ids': adapter_ids}
    _L0_cond_all = _L0_cond_setup()
    _L0_cond_in = {k: v for k, v in _L0_cond_all.items() if k in ('A', 'B')}
    del _L0_cond_all

    def _L0_ffn_setup():
        import jax, jax.numpy as jnp
        import numpy as np

        @jax.custom_vjp
        def ste_sign(w):
            return jnp.sign(w)

        def _ste_fwd(w):
            return (jnp.sign(w), w)

        def _ste_bwd(w, g):
            mask = ((w > -1) & (w < 1)).astype(g.dtype)
            return (g * mask,)
        ste_sign.defvjp(_ste_fwd, _ste_bwd)
        key = jax.random.key(seed)
        k = jax.random.split(key, 6)
        B, S, H, O, E = (4, 1024, 2048, 2048, 8)
        return {'x': jax.random.normal(k[0], (B, S, H), dtype=jnp.float32), 'weight': jax.random.normal(k[1], (O, H), dtype=jnp.float32) * 0.02, 'bias': jax.random.normal(k[2], (O,), dtype=jnp.float32) * 0.02, 'gate_w': jax.random.normal(k[3], (E, H), dtype=jnp.float32) * 0.02, 'in_channel_scale': jax.random.normal(k[4], (E, H), dtype=jnp.float32), 'out_channel_scale': jax.random.normal(k[5], (E, O), dtype=jnp.float32)}
    _L0_ffn_all = _L0_ffn_setup()
    _L0_ffn_in = {k: v for k, v in _L0_ffn_all.items() if k in ('weight', 'bias', 'gate_w', 'in_channel_scale', 'out_channel_scale')}
    del _L0_ffn_all
    return {'x': x, 'itok_B_3_7': itok_B_3_7, 'L0_cond_A': _L0_cond_in['A'], 'L0_cond_B': _L0_cond_in['B'], 'L0_ffn_weight': _L0_ffn_in['weight'], 'L0_ffn_bias': _L0_ffn_in['bias'], 'L0_ffn_gate_w': _L0_ffn_in['gate_w'], 'L0_ffn_in_channel_scale': _L0_ffn_in['in_channel_scale'], 'L0_ffn_out_channel_scale': _L0_ffn_in['out_channel_scale']}

def reference(x, itok_B_3_7, L0_cond_A, L0_cond_B, L0_ffn_weight, L0_ffn_bias, L0_ffn_gate_w, L0_ffn_in_channel_scale, L0_ffn_out_channel_scale):
    import jax
    import jax.numpy as jnp

    def _L0_cond_ref(x, A, B, adapter_ids):
        import jax, jax.numpy as jnp
        import numpy as np
        RANK = 16
        ALPHA = 16.0
        SCALING = ALPHA / RANK
        N_ADAPTERS = 8
        IN_F = 2048
        OUT_F = 2048
        BATCH = 4
        SEQ = 1024
        B_sel = B[adapter_ids]
        A_sel = A[adapter_ids]
        Bx = jnp.einsum('bni,bri->bnr', x, B_sel)
        out = jnp.einsum('bnr,bor->bno', Bx, A_sel)
        return out * SCALING

    def _L0_ffn_ref(x, weight, bias, gate_w, in_channel_scale, out_channel_scale):
        import jax, jax.numpy as jnp
        import numpy as np

        @jax.custom_vjp
        def ste_sign(w):
            return jnp.sign(w)

        def _ste_fwd(w):
            return (jnp.sign(w), w)

        def _ste_bwd(w, g):
            mask = ((w > -1) & (w < 1)).astype(g.dtype)
            return (g * mask,)
        ste_sign.defvjp(_ste_fwd, _ste_bwd)
        B, S, H = x.shape
        xf = x.reshape(-1, H)
        router_logits = xf @ gate_w.T
        routing = jax.nn.softmax(router_logits.astype(jnp.float32), axis=1).astype(x.dtype)
        in_scale = routing @ in_channel_scale
        out_scale = routing @ out_channel_scale
        wb = ste_sign(weight)
        out = xf * in_scale @ wb.T * out_scale + bias
        return out.reshape(B, S, -1)
    x = x + _L0_ffn_ref(_L0_cond_ref(x, L0_cond_A, L0_cond_B, itok_B_3_7), L0_ffn_weight, L0_ffn_bias, L0_ffn_gate_w, L0_ffn_in_channel_scale, L0_ffn_out_channel_scale)
    return x

_drawn_inputs = setup_inputs


def setup_inputs(seed=0):
    import zlib

    import numpy as np

    out = dict(_drawn_inputs(seed))
    spreads = {}
    factors = {'L0_ffn_bias': 2.977}
    for name, (base, spread) in spreads.items():
        noise = np.random.default_rng([zlib.crc32(name.encode()), seed]).standard_normal(out[name].shape)
        drawn = base * np.exp(spread * noise) if base else spread * noise
        out[name] = jnp.asarray(drawn.astype(out[name].dtype))
    for name, factor in factors.items():
        out[name] = (out[name] * factor).astype(out[name].dtype)
    return out
```

```python
from contextlib import ExitStack

import concourse.bass as bass
from concourse import mybir


P = 128
F32 = mybir.dt.float32
F16 = mybir.dt.float16
BF16 = mybir.dt.bfloat16
I32 = mybir.dt.int32
ALU = mybir.AluOpType
ACT = mybir.ActivationFunctionType
AX = mybir.AxisListType


def adaln_ffn(nc, x, ids, lora_a, lora_b, weight, bias, gate_w, ics, ocs, out):
    NB, S, H = x.shape
    NA, O, R = lora_a.shape
    E = gate_w.shape[0]
    C = H // P
    T = S // P
    QW = 512
    Q = O // QW
    CQ = C // Q
    RE = R * E
    BW = R + E
    PARTS = 3
    K2 = PARTS * PARTS * E
    UN = Q * T
    WT = O // P
    HALF = C // 2
    OSB = 2
    XTB = 4
    assert RE == P and NB * R == P and H == O and Q * CQ == C and CQ == T == 4 and NB == 8

    x_v = x.rearrange("b (t p) h -> b p t h", p=P)
    out_v = out.rearrange("b (t p) h -> b p t h", p=P)
    a_v = lora_a.rearrange("a (p c) r -> a p (c r)", c=C)
    w_v = weight.rearrange("(w p) h -> w p h", p=P)
    gate_v = gate_w.rearrange("e (p c) -> p e c", c=C)
    ics_v = ics.rearrange("e (p c) -> p e c", c=C)

    with ExitStack() as ctx:
        def sb(name, shape, dt):
            return ctx.enter_context(nc.sbuf_tensor(name, shape, dt))

        def ps(name, shape, dt):
            return ctx.enter_context(nc.psum_tensor(name, shape, dt))

        def sem(name):
            return ctx.enter_context(nc.semaphore(name))

        wt = sb("sign_w_T", [P, C, O], F16)
        xb = sb("x_rows", [P, 2, T, H], F32)
        bc = sb("bx_logit_weights", [P, C, NB, BW], F32)
        bcur = sb("bx_logit_weights_now", [P, 2, C, BW], F32)
        asel = sb("a_selected", [P, NB, C, R], F32)
        icss = sb("in_scale_scaled", [P, E, C], F32)
        gate = sb("gate_cols", [P, E, C], F32)
        g = sb("g_parts", [P, 2, 2, C, RE], F16)
        gtmp = sb("g_full", [P, 2, CQ, RE], F32)
        m = sb("m_rows", [P, O], F32)
        xT = sb("x_T", [P, XTB, CQ, P], F32)
        biasb = sb("bias_rows", [P, O], F32)
        oparts = sb("out_scale_stack", [K2, O], BF16)
        pT = sb("p_T", [P, 2, T, P], F32)
        rT = sb("r_T", [K2, 2, T, P], BF16)
        work = sb("work", [P, (OSB + 2) * QW], F32)
        oscale = work[:, 0:OSB * QW].rearrange("p (n q) -> p n q", n=OSB)
        scaled = work[:, OSB * QW:(OSB + 2) * QW].rearrange("p (n q) -> p n q", n=2)
        sgn = work[:, 0:H].bitcast(F16).rearrange("p (n h) -> p n h", n=2)
        bsel = m
        acols = bc[:].rearrange("p c b w -> p (c b w)")[:, 0:C * P].rearrange("p (c n) -> p c n", c=C)
        ident = sb("ident", [P, P], F32)
        ident16 = sb("ident16", [P, P], F16)
        identb = sb("identb", [P, P], BF16)
        rw = sb("b_to_weights", [P, NB, BW], F32)
        ga = sb("gate_a", [P, E], F32)
        diag = sb("batch_diag", [P, NB], F32)
        absmax = sb("absmax", [P, NB + 1], F32)
        allmax = sb("allmax", [P, NB + 1], F32)
        pow2 = sb("pow2", [P, NB + 1], F32)
        upscale = sb("upscale", [P, NB + 1], F32)
        unscale = sb("unscale", [P, NB], F32)
        unow = sb("unscale_now", [P, 2], F32)
        idrow = sb("id_row", [1, NB], I32)
        bxl = sb("bx_logits", [P, T, BW], F32)
        mx = sb("logit_max", [P, T], F32)
        ex = sb("exps", [P, T, E], F32)
        sm = sb("exp_sum", [P, T], F32)
        rs = sb("exp_sum_inv", [P, T], F32)
        rt = sb("routing", [P, T, E], F32)
        rd = sb("routing_rest", [P, T, E], F32)
        rparts = sb("routing_parts", [P, T, PARTS, PARTS, E], BF16)
        pn = sb("p_rows", [P, T, R, E], F32)
        op16 = g[0:E].rearrange("p a b c n -> p (a b c n)")[:, 0:PARTS * O].bitcast(BF16).rearrange(
            "p (i o) -> p i o", i=PARTS)
        ofull = xT[0:E, :, :, :].rearrange("p n c q -> p (n c q)")

        psM = ps("ps_m", [P, 2, QW], F32)
        psT = ps("ps_x_T", [P, 2, QW], F32)
        psPre = ps("ps_pre", [P, QW], F32)
        psOs = ps("ps_oscale", [P, QW], F32)
        psP = ps("ps_p_T", [P, T, P], F32)
        psS = ps("ps_small", [P, QW], F32)
        acc = psS[:, 0:T * BW].rearrange("p (t w) -> p t w", t=T)
        psR = psS[:, QW // 2:QW].bitcast(BF16).rearrange("p (t n) -> p t n", t=T)
        psW = [psPre[:].bitcast(F16).rearrange("p (c n) -> p c n", c=HALF),
               psOs[:].bitcast(F16).rearrange("p (c n) -> p c n", c=HALF)]

        ids_in = sem("ids_in")
        small_in = sem("small_in")
        bias_in = sem("bias_in")
        ocs_in = sem("ocs_in")
        a_in = sem("a_in")
        b_in = sem("b_in")
        w_in = [sem(f"w_in{i}") for i in range(4)]
        x_in = [[sem(f"x_in{i}_{q}") for q in range(Q)] for i in range(2)]
        stored = [[sem(f"stored{i}_{q}") for q in range(Q)] for i in range(2)]
        ostack_in = sem("ostack_in")
        ident_ok = sem("ident_ok")
        opart_ok = sem("opart_ok")
        max_ok = sem("max_ok")
        allmax_ok = sem("allmax_ok")
        acols_ok = sem("acols_ok")
        ga_done = sem("ga_done")
        prep = sem("prep")
        rw_ok = sem("rw_ok")
        scale_ok = sem("scale_ok")
        ascaled = sem("a_scaled")
        bcmm_done = sem("bcmm_done")
        bc_ok = sem("bc_ok")
        sign_ok = sem("sign_ok")
        wtr_done = sem("wtr_done")
        wt_ok = sem("wt_ok")
        bcur_ok = sem("bcur_ok")
        gfull_ok = sem("gfull_ok")
        ghigh_ok = sem("ghigh_ok")
        glow_ok = sem("glow_ok")
        xtr_done = sem("xtr_done")
        xT_ok = sem("xT_ok")
        bx_done = sem("bx_done")
        m_done = sem("m_done")
        m_ok = sem("m_ok")
        chain = sem("chain")
        exp_in = sem("exp_in")
        exp_ok = sem("exp_ok")
        rp_ok = sem("rp_ok")
        pr_done = sem("pr_done")
        pT_ok = sem("pT_ok")
        rT_ok = sem("rT_ok")
        pre_done = sem("pre_done")
        os_done = sem("os_done")
        oscale_ok = sem("oscale_ok")
        mul_done = sem("mul_done")
        xbias_ok = sem("xbias_ok")
        out_ok = sem("out_ok")

        block = ctx.enter_context(nc.Block())

        UNITS = [[2 * s, 2 * s + 1] if s < 6 else [s + 6] if s < 10 else [] for s in range(UN)]
        SOFT = 10
        PTR = 13

        class Step:
            def __init__(self, j, par):
                self.j, self.par = j, par

            def at(self, per, c):
                if isinstance(self.j, int):
                    return per * (2 * self.j + self.par) + c
                return self.j * (2 * per) + (per * self.par + c)

            def half(self, per, c):
                return self.j * per + c

        def steps(eng, body):
            with eng.Fori(0, NB // 2 - 1) as j:
                body(Step(j, 0), True, True)
                body(Step(j, 1), True, True)
            body(Step(NB // 2 - 1, 0), True, False)
            body(Step(NB // 2 - 1, 1), False, False)

        @block.sync
        def _(sp):
            def load_x(b, par, q, who):
                return sp.dma_start(xb[:, par, :, q * QW:(q + 1) * QW],
                                    who[:, :, q * QW:(q + 1) * QW]).then_inc(x_in[par][q], 16)

            for w in range(WT):
                if w >= 4:
                    sp.wait_ge(sign_ok, w - 3)
                sp.dma_start(xb[:, 1, w % 4, :], w_v[w]).then_inc(w_in[w % 4], 16)
                if w % 4 == 3:
                    load_x(0, 0, w // 4, x_v[0])
                if w == 3:
                    sp.wait_ge(opart_ok, 3)
                    for i in range(PARTS):
                        for jj in range(PARTS):
                            row = (i * PARTS + jj) * E
                            src = op16[:, jj, :]
                            sp.dma_start(oparts[row:row + E, :], src).then_inc(ostack_in, 16)
            sp.wait_ge(sign_ok, WT)
            for q in range(Q):
                load_x(1, 1, q, x_v[1])

            def body(k, ahead, ahead2):
                b = k.at(1, 0)
                src_out = out_v[b] if isinstance(b, int) else out_v[bass.ds(b, 1)].rearrange("b p t h -> (b p) t h")

                def reload(q):
                    b2 = k.at(1, 2)
                    src = x_v[b2] if isinstance(b2, int) else x_v[bass.ds(b2, 1)].rearrange("b p t h -> (b p) t h")
                    sp.wait_ge(stored[k.par][q], k.half(16, 16))
                    load_x(b2, k.par, q, src)

                for q in range(Q):
                    sp.wait_ge(out_ok, k.at(UN, T * (q + 1)))
                    sp.dma_start(src_out[:, :, q * QW:(q + 1) * QW],
                                 xb[:, k.par, :, q * QW:(q + 1) * QW]).then_inc(stored[k.par][q], 16)
                    if ahead2 and q >= 1:
                        reload(q - 1)
                if ahead2:
                    reload(Q - 1)

            steps(sp, body)
            for par in range(2):
                for q in range(Q):
                    sp.wait_ge(stored[par][q], 16 * (NB // 2))


        @block.gpsimd
        def _(pool):
            nc.gpsimd.memset(ident[:], 0.0).then_inc(ident_ok, 1)
            pool.wait_ge(ident_ok, 1)
            nc.gpsimd.affine_select(out=ident[:], in_=ident[:], compare_op=ALU.not_equal, fill=1.0, base=0,
                                    pattern=[[-1, P]], channel_multiplier=1).then_inc(ident_ok, 1)
            pool.wait_ge(ident_ok, 2)
            nc.gpsimd.tensor_copy(ident16[:], ident[:]).then_inc(ident_ok, 1)
            nc.gpsimd.tensor_copy(identb[:], ident[:]).then_inc(ident_ok, 1)

            pool.wait_ge(a_in, 16 * NB)
            nc.gpsimd.tensor_copy(acols.rearrange("p c (b r) -> p b c r", b=NB), asel[:]).then_inc(acols_ok, 1)
            pool.wait_ge(max_ok, 2)
            nc.gpsimd.partition_all_reduce(allmax[:], absmax[:], P, bass.bass_isa.ReduceOp.max).then_inc(allmax_ok, 1)

            pool.wait_ge(scale_ok, 1)
            pool.wait_ge(ga_done, 1)
            nc.gpsimd.tensor_tensor(icss[:], icss[:], upscale[:, NB:NB + 1].unsqueeze(2).broadcast_to([P, E, C]),
                                    ALU.mult).then_inc(ascaled, 1)
            nc.gpsimd.tensor_tensor(asel[:].rearrange("p b c r -> p b (c r)"),
                                    asel[:].rearrange("p b c r -> p b (c r)"),
                                    upscale[:, 0:NB].unsqueeze(2).broadcast_to([P, NB, C * R]),
                                    ALU.mult).then_inc(ascaled, 1)
            pool.wait_ge(ascaled, 2)

            def g_full(b, par, grp, gate_count):
                a = asel[:, b] if isinstance(b, int) else asel[:, bass.ds(b, 1)].rearrange("p b c r -> p (b c) r")
                a = a[:, grp * CQ:(grp + 1) * CQ, :].unsqueeze(3).broadcast_to([P, CQ, R, E])
                for c in range(CQ):
                    cc = grp * CQ + c
                    i = nc.gpsimd.tensor_tensor(gtmp[:, grp % 2, c].rearrange("p (r e) -> p r e", e=E), a[:, c],
                                                icss[:, :, cc].unsqueeze(1).broadcast_to([P, R, E]), ALU.mult)
                i.then_inc(gfull_ok, 1)

            def take_weights(b, par):
                src = bc[:, :, b, :] if isinstance(b, int) else bc[:, :, bass.ds(b, 1), :].rearrange("p c b w -> p c (b w)")
                nc.gpsimd.tensor_copy(bcur[:, par], src).then_inc(bcur_ok, 1)
                u = unscale[:, b:b + 1] if isinstance(b, int) else unscale[:, bass.ds(b, 1)]
                nc.gpsimd.tensor_copy(unow[:, par:par + 1], u).then_inc(bcur_ok, 1)

            for b in range(2):
                for grp in range(Q):
                    if 4 * b + grp >= 2:
                        pool.wait_ge(glow_ok, 4 * b + grp - 1)
                    g_full(b, b % 2, grp, None)
                    if 4 * b + grp == 1:
                        pool.wait_ge(bc_ok, C // 2)
                        take_weights(0, 0)
                        take_weights(1, 1)
            pool.wait_ge(bias_in, 16)

            def body(k, ahead, ahead2):
                if ahead2:
                    pool.wait_ge(bx_done, k.at(UN, UN))
                    pool.wait_ge(m_ok, k.at(Q, Q))
                    take_weights(k.at(1, 2), k.par)
                for s in range(UN):
                    q, t = divmod(s, T)
                    if s == 0:
                        pool.wait_ge(xtr_done, k.at(UN, UN))
                    xs = xb[:, k.par, t, q * QW:(q + 1) * QW]
                    nc.gpsimd.tensor_tensor(xs, xs, biasb[:, q * QW:(q + 1) * QW], ALU.add).then_inc(xbias_ok, 1)
                    if ahead2 and t == 1:
                        pool.wait_ge(glow_ok, k.at(Q, 2 * Q + q - 1))
                        g_full(k.at(1, 2), k.par, q, None)

            steps(pool, body)

        @block.scalar
        def _(act):
            act.dma_start(idrow[:], ids.rearrange("(a b) -> a b", a=1)).then_inc(ids_in, 16)
            act.dma_start(gate[:], gate_v).then_inc(small_in, 16)
            act.dma_start(icss[:], ics_v).then_inc(small_in, 16)
            act.dma_start(ofull, ocs).then_inc(ocs_in, 16)
            act.wait_ge(ids_in, 16)
            for b in range(NB):
                a = act.value_load(idrow[0:1, b:b + 1], min_val=0, max_val=NA - 1)
                act.dma_start(asel[:, b].rearrange("p c r -> p (c r)"),
                              a_v[bass.ds(a, 1)].rearrange("a p n -> (a p) n")).then_inc(a_in, 16)
                act.dma_start(bsel[b * R:(b + 1) * R, :],
                              lora_b[bass.ds(a, 1)].rearrange("a r i -> (a r) i")).then_inc(b_in, 16)
            act.dma_start(biasb[:], bias.rearrange("(a o) -> a o", a=1).broadcast_to([P, O])).then_inc(bias_in, 16)

            def g_high(par, grp):
                nc.scalar.activation(g[:, par, 0, grp * CQ:(grp + 1) * CQ, :], gtmp[:, grp % 2], ACT.Copy).then_inc(ghigh_ok, 1)

            def evac_x(u, count, tr, free):
                act.wait_ge(xtr_done, tr)
                if free is not None:
                    act.wait_ge(bx_done, free)
                nc.scalar.activation(xT[:, u % XTB], psT[:, u % 2, :].rearrange("p (c n) -> p c n", c=CQ), ACT.Copy).then_inc(xT_ok, 1)

            def evac_m(par, q, count, used):
                act.wait_ge(m_done, count)
                if used is not None:
                    act.wait_ge(pre_done, used)
                nc.scalar.activation(m[:, q * QW:(q + 1) * QW], psM[:, q % 2, :], ACT.Copy, scale=unow[:, par:par + 1]).then_inc(m_ok, 1)

            def exps(count):
                act.wait_ge(exp_in, count)
                nc.scalar.activation(ex[:], ex[:], ACT.Exp).then_inc(exp_ok, 1)

            def evac_r(par, count, used):
                act.wait_ge(pr_done, count)
                if used is not None:
                    act.wait_ge(os_done, used)
                nc.scalar.activation(rT[:, par], psR[0:K2], ACT.Copy).then_inc(rT_ok, 1)

            for w in range(WT):
                act.wait_ge(w_in[w % 4], 16 * (w // 4 + 1))
                if w >= 2:
                    act.wait_ge(wtr_done, 2 * (w - 1))
                nc.scalar.activation(sgn[:, w % 2, :], xb[:, 1, w % 4, :], ACT.Sign).then_inc(sign_ok, 1)
                if w < 8:
                    if w == 0:
                        act.wait_ge(ostack_in, 16 * K2 // E)
                    act.wait_ge(gfull_ok, w + 1)
                    g_high(w // 4, w % 4)
                q, t = divmod(w, 4)
                if t == 3:
                    for tt in range(T):
                        u = q * T + tt
                        evac_x(u, None, u + 1, u - XTB + 1 if u >= XTB else None)
                    if q == 0:
                        act.wait_ge(bcmm_done, C // 2)
                    evac_m(0, q, q + 1, None)
            exps(1)
            evac_r(0, 1, None)

            def body(k, ahead, ahead2):
                for s in range(UN):
                    q, t = divmod(s, T)
                    act.wait_ge(os_done, k.at(UN, s + 1))
                    act.wait_ge(mul_done, k.at(UN, s + 1))
                    nc.scalar.activation(oscale[:, s % OSB, :], psOs[:], ACT.Copy).then_inc(oscale_ok, 1)
                    if ahead:
                        for u in UNITS[s]:
                            evac_x(u, None, k.at(UN, UN + u + 1), k.at(UN, UN + u - XTB + 1))
                    if ahead2 and t == 2:
                        act.wait_ge(gfull_ok, k.at(Q, 2 * Q + q + 1))
                        if q == 0:
                            act.wait_ge(m_done, k.at(Q, Q))
                        g_high(k.par, q)
                    if ahead:
                        if s == SOFT:
                            exps(k.at(1, 2))
                        if s == PTR:
                            evac_r(1 - k.par, k.at(1, 2), k.at(UN, 1))
                        if t == 3:
                            evac_m(1 - k.par, q, k.at(Q, Q + q + 1), k.at(UN, s + 1))

            steps(act, body)

        @block.vector
        def _(dve):
            V = nc.vector
            dve.wait_ge(ocs_in, 16)
            V.tensor_copy(op16[:, 0, :], ofull).then_inc(opart_ok, 1)
            dve.wait_ge(opart_ok, 1)
            V.tensor_tensor(ofull, ofull, op16[:, 0, :], ALU.subtract).then_inc(prep, 1)
            dve.wait_ge(prep, 1)
            V.tensor_copy(op16[:, 1, :], ofull).then_inc(opart_ok, 1)
            dve.wait_ge(opart_ok, 2)
            V.tensor_tensor(op16[:, 2, :], ofull, op16[:, 1, :], ALU.subtract).then_inc(opart_ok, 1)
            dve.wait_ge(small_in, 32)
            V.tensor_reduce(absmax[:, NB:NB + 1], icss[:].rearrange("p e c -> p (e c)"), AX.X, ALU.max,
                            apply_absolute_value=True).then_inc(max_ok, 1)
            dve.wait_ge(a_in, 16 * NB)
            V.tensor_reduce(absmax[:, 0:NB], asel[:].rearrange("p b c r -> p b (c r)"), AX.X, ALU.max,
                            apply_absolute_value=True).then_inc(max_ok, 1)
            dve.wait_ge(ident_ok, 4)
            V.tensor_reduce(diag[:], ident[:].rearrange("p (b r) -> p b r", r=R), AX.X, ALU.add).then_inc(prep, 1)
            V.tensor_copy(rw[:, :, 0:R], ident[:].rearrange("p (b r) -> p b r", r=R)).then_inc(rw_ok, 1)
            dve.wait_ge(allmax_ok, 1)
            V.tensor_scalar(allmax[:], allmax[:], 2.0 ** -100, None, ALU.max).then_inc(prep, 1)
            dve.wait_ge(prep, 3)
            V.tensor_scalar(pow2[:].bitcast(I32), allmax[:].bitcast(I32), 0x7F800000, None,
                            ALU.bitwise_and).then_inc(prep, 1)
            dve.wait_ge(prep, 4)
            V.reciprocal(upscale[:], pow2[:]).then_inc(prep, 1)
            V.tensor_scalar(unscale[:], pow2[:, 0:NB], pow2[:, NB:NB + 1], 2.0 ** -13, ALU.mult, ALU.mult).then_inc(prep, 1)
            dve.wait_ge(prep, 5)
            V.tensor_scalar(upscale[:, 0:NB], upscale[:, 0:NB], 2.0 ** 7, None, ALU.mult).then_inc(prep, 1)
            V.tensor_scalar(upscale[:, NB:NB + 1], upscale[:, NB:NB + 1], 2.0 ** 6, None, ALU.mult).then_inc(scale_ok, 1)
            dve.wait_ge(ga_done, 1)
            V.tensor_copy(ga[:], psP[:, 0, 0:E]).then_inc(prep, 1)
            dve.wait_ge(prep, 8)
            V.tensor_tensor(rw[:, :, R:BW], ga[:].unsqueeze(1).broadcast_to([P, NB, E]),
                            diag[:].unsqueeze(2).broadcast_to([P, NB, E]), ALU.mult).then_inc(rw_ok, 1)
            for c in range(0, C, 2):
                dve.wait_ge(bcmm_done, c // 2 + 1)
                V.tensor_copy(bc[:, c:c + 2].rearrange("p c b w -> p c (b w)"),
                              psM[:, (c // 2) % 2, 0:2 * NB * BW].rearrange("p (c n) -> p c n", c=2)).then_inc(bc_ok, 1)

            def g_low(par, grp, count):
                dve.wait_ge(ghigh_ok, count)
                sl = slice(grp * CQ, (grp + 1) * CQ)
                V.tensor_tensor(g[:, par, 1, sl, :], gtmp[:, grp % 2], g[:, par, 0, sl, :], ALU.subtract).then_inc(glow_ok, 1)

            CH = 9

            def softmax(b, part):
                def link(i, c):
                    i.then_inc(chain, 1)
                    dve.wait_ge(chain, b(CH, c))

                if part == 0:
                    dve.wait_ge(bx_done, b(UN, UN))
                    link(V.tensor_copy(bxl[:], acc), 1)
                    link(V.tensor_reduce(mx[:], bxl[:, :, R:BW], AX.X, ALU.max), 2)
                    V.tensor_tensor(ex[:], bxl[:, :, R:BW], mx[:].unsqueeze(2).broadcast_to([P, T, E]),
                                    ALU.subtract).then_inc(exp_in, 1)
                if part == 1:
                    dve.wait_ge(exp_ok, b(1, 1))
                    link(V.tensor_reduce(sm[:], ex[:], AX.X, ALU.add), 3)
                    link(V.reciprocal(rs[:], sm[:]), 4)
                    link(V.tensor_tensor(rt[:], ex[:], rs[:].unsqueeze(2).broadcast_to([P, T, E]), ALU.mult), 5)
                    V.tensor_tensor(pn[:], bxl[:, :, 0:R].unsqueeze(3).broadcast_to([P, T, R, E]),
                                    rt[:].unsqueeze(2).broadcast_to([P, T, R, E]), ALU.mult).then_inc(rp_ok, 1)
                if part == 2:
                    for i in range(PARTS):
                        src = rt if i == 0 else rd
                        for jj in range(PARTS):
                            ins = V.tensor_copy(rparts[:, :, i, jj, :], src[:])
                            if i == PARTS - 1:
                                if jj == PARTS - 1:
                                    ins.then_inc(rp_ok, 1)
                            elif jj == 0:
                                ins.then_inc(chain, 1)
                        if i < PARTS - 1:
                            dve.wait_ge(chain, b(CH, 6 + 2 * i))
                            link(V.tensor_tensor(rd[:], src[:], rparts[:, :, i, 0, :], ALU.subtract), 7 + 2 * i)

            def evac_p(par, count, used):
                dve.wait_ge(pr_done, count)
                if used is not None:
                    dve.wait_ge(pre_done, used)
                V.tensor_copy(pT[:, par], psP[:]).then_inc(pT_ok, 1)

            for w in range(WT):
                if w < 8:
                    g_low(w // 4, w % 4, w + 1)
                for half in range(2):
                    dve.wait_ge(wtr_done, 2 * w + half + 1)
                    V.tensor_copy(wt[:, half * HALF:(half + 1) * HALF, w * P:(w + 1) * P], psW[half]).then_inc(wt_ok, 1)
            fixed = lambda per, c: c
            softmax(fixed, 0)
            softmax(fixed, 1)
            softmax(fixed, 2)
            evac_p(0, 1, None)

            def body(k, ahead, ahead2):
                for s in range(UN):
                    q, t = divmod(s, T)
                    n = s % 2
                    dve.wait_ge(pre_done, k.at(UN, s + 1))
                    dve.wait_ge(oscale_ok, k.at(UN, s + 1))
                    V.tensor_tensor(scaled[:, n], psPre[:], oscale[:, s % OSB], ALU.mult).then_inc(mul_done, 1)
                    dve.wait_ge(mul_done, k.at(UN, s + 3))
                    dve.wait_ge(xbias_ok, k.at(UN, s + 1))
                    xs = xb[:, k.par, t, q * QW:(q + 1) * QW]
                    V.tensor_tensor(xs, xs, scaled[:, n], ALU.add).then_inc(out_ok, 1)
                    if ahead2 and t == 3:
                        g_low(k.par, q, k.at(Q, 2 * Q + q + 1))
                    if ahead:
                        nxt = lambda per, c: k.at(per, per + c)
                        if SOFT <= s < SOFT + 3:
                            softmax(nxt, s - SOFT)
                        if s == PTR:
                            evac_p(1 - k.par, k.at(1, 2), k.at(UN, 1))

            for i in range(OSB):
                V.memset(mx[:, i:i + 1], 0.0).then_inc(mul_done, 1)
            steps(dve, body)

        @block.tensor
        def _(pe):
            mm = nc.tensor.matmul

            def transpose_x(u, par, loaded, free):
                q, t = divmod(u, T)
                if loaded is not None:
                    pe.wait_ge(x_in[par][q], loaded)
                if free is not None:
                    pe.wait_ge(xT_ok, free)
                for c in range(CQ):
                    i = nc.tensor.transpose(psT[:, u % 2, c * P:(c + 1) * P],
                                            xb[:, par, t, q * QW + c * P:q * QW + (c + 1) * P], ident[:])
                i.then_inc(xtr_done, 1)

            def product_x(u, par, ready, free):
                q, t = divmod(u, T)
                if free is not None:
                    pe.wait_ge(rT_ok, free)
                pe.wait_ge(xT_ok, ready)
                for c in range(CQ):
                    cc = q * CQ + c
                    i = mm(acc[:, t, :], xT[:, u % XTB, c, :], bcur[:, par, cc, :],
                           start=(u == 0 and c == 0), stop=(cc == C - 1), skip_group_check=True)
                i.then_inc(bx_done, 1)

            def product_m(q, t, par, free):
                if t == 0 and free is not None:
                    pe.wait_ge(m_ok, free)
                for c in range(t * CQ, (t + 1) * CQ):
                    for part in range(2):
                        i = mm(psM[:, q % 2, :], g[:, par, part, c, :], wt[:, c, q * QW:(q + 1) * QW],
                               start=(c == 0 and part == 0), stop=(c == C - 1 and part == 1))
                if t == T - 1:
                    i.then_inc(m_done, 1)

            def transpose_pr(ready):
                pe.wait_ge(rp_ok, ready)
                for t in range(T):
                    nc.tensor.transpose(psP[:, t, :], pn[:, t].rearrange("p r e -> p (r e)"), ident[:])
                for t in range(T):
                    i = nc.tensor.transpose(psR[0:K2, t, :], rparts[:, t].rearrange("p i j e -> p (i j e)"), identb[:])
                i.then_inc(pr_done, 1)

            pe.wait_ge(small_in, 32)
            pe.wait_ge(acols_ok, 1)
            for c in range(C):
                i = mm(psP[:, 0, 0:E], acols[:, c, :], gate[:, :, c], start=(c == 0), stop=(c == C - 1))
            i.then_inc(ga_done, 1)
            pe.wait_ge(b_in, 16 * NB)
            pe.wait_ge(rw_ok, 2)
            for c in range(C):
                if c >= 4 and c % 2 == 0:
                    pe.wait_ge(bc_ok, c // 2 - 1)
                i = mm(psM[:, (c // 2) % 2, (c % 2) * NB * BW:(c % 2 + 1) * NB * BW], bsel[:, c * P:(c + 1) * P],
                       rw[:].rearrange("p b w -> p (b w)"), start=(c % 2 == 0), stop=True, skip_group_check=True)
                if c % 2 == 1:
                    i.then_inc(bcmm_done, 1)
            pe.wait_ge(bc_ok, C // 2)
            for w in range(WT):
                pe.wait_ge(sign_ok, w + 1)
                for half in range(2):
                    if w >= 1:
                        pe.wait_ge(wt_ok, 2 * (w - 1) + half + 1)
                    for c in range(HALF):
                        i = nc.tensor.transpose(psW[half][:, c, :],
                                                sgn[:, w % 2, half * HALF + c:H:C], ident16[:])
                    i.then_inc(wtr_done, 1)
                if w % 4 == 3:
                    q = w // 4
                    if q == 0:
                        pe.wait_ge(bcur_ok, 2)
                    for t in range(T):
                        u = q * T + t
                        transpose_x(u, 0, 16 if t == 0 else None, u - 1 if u >= 2 else None)
                        product_x(u, 0, u + 1, None)
                    pe.wait_ge(wt_ok, 2 * (w + 1))
                    if q == 0:
                        pe.wait_ge(glow_ok, Q)
                    for t in range(T):
                        product_m(q, t, 0, q - 1 if q >= 2 else None)
            transpose_pr(2)

            def body(k, ahead, ahead2):
                for s in range(UN):
                    q, t = divmod(s, T)
                    sl = slice(q * QW, (q + 1) * QW)
                    if s == 0:
                        pe.wait_ge(pT_ok, k.at(1, 1))
                    if t == 0:
                        pe.wait_ge(m_ok, k.at(Q, q + 1))
                    pe.wait_ge(mul_done, k.at(UN, s + 2))
                    mm(psPre[:], pT[:, k.par, t, :], m[:, sl], start=True, stop=True).then_inc(pre_done, 1)
                    if s == 0:
                        pe.wait_ge(rT_ok, k.at(1, 1))
                    mm(psOs[:], rT[:, k.par, t, :], oparts[:, sl], start=True, stop=True).then_inc(os_done, 1)
                    if ahead:
                        for u in UNITS[s]:
                            uq, ut = divmod(u, T)
                            transpose_x(u, 1 - k.par,
                                        (k.half(16, 16) if k.par == 0 else k.half(16, 32)) if ut == 0 else None,
                                        k.at(UN, UN + u - 1))
                        if s == 0:
                            pe.wait_ge(glow_ok, k.at(Q, 2 * Q))
                            pe.wait_ge(bcur_ok, k.at(2, 4))
                        product_m(q, t, 1 - k.par, k.at(Q, Q + q - 1))
                        for u in UNITS[s]:
                            product_x(u, 1 - k.par, k.at(UN, UN + u + 1), k.at(1, 1) if u == 0 else None)
                        if s == PTR:
                            transpose_pr(k.at(2, 4))

            pe.wait_ge(ostack_in, 16 * K2 // E)
            steps(pe, body)


_INS = ['x', 'itok_B_3_7', 'L0_cond_A', 'L0_cond_B', 'L0_ffn_weight', 'L0_ffn_bias', 'L0_ffn_gate_w',
        'L0_ffn_in_channel_scale', 'L0_ffn_out_channel_scale']


def kernel(**inputs):
    import numpy as _np
    import concourse.bacc as _bacc
    from concourse import mybir as _mybir
    from concourse.bass_utils import run_bass_kernel_spmd as _run

    nc = _bacc.Bacc("TRN2", target_bir_lowering=False, num_devices=1, dynamic_dma_scratch_size=1024)
    arrays, args = {}, []
    for name in _INS:
        a = _np.ascontiguousarray(inputs[name])
        arrays[f"in_{name}_dram"] = a
        args.append(nc.dram_tensor(f"in_{name}_dram", a.shape, _mybir.dt.from_np(a.dtype), kind="ExternalInput").ap())
    shape = inputs['x'].shape
    args.append(nc.dram_tensor("out_0_dram", shape, _mybir.dt.float32, kind="ExternalOutput").ap())
    adaln_ffn(nc, *args)
    r = _run(nc, [arrays], core_ids=[0])
    return r.results[0]["out_0_dram"]
```

```python
from contextlib import ExitStack

import concourse.bass as bass
from concourse import mybir


P = 128
F32 = mybir.dt.float32
F16 = mybir.dt.float16
BF16 = mybir.dt.bfloat16
I32 = mybir.dt.int32
ALU = mybir.AluOpType
ACT = mybir.ActivationFunctionType
AX = mybir.AxisListType


def adaln_ffn(nc, x, ids, lora_a, lora_b, weight, bias, gate_w, ics, ocs, out):
    NB, S, H = x.shape
    NA, O, R = lora_a.shape
    E = gate_w.shape[0]
    C = H // P
    T = S // P
    QW = 512
    Q = O // QW
    CQ = C // Q
    RE = R * E
    BW = R + E
    CT = 32
    PARTS = 3
    K2 = PARTS * PARTS * E
    UN = Q * T
    WT = O // P
    HALF = C // 2
    OSB = 2
    XTB = 4
    assert CQ * CT == P and BW <= CT and XTB == CQ
    assert RE == P and NB * R == P and H == O and Q * CQ == C and CQ == T == 4 and NB == 8

    x_v = x.rearrange("b (t p) h -> b p t h", p=P)
    out_v = out.rearrange("b (t p) h -> b p t h", p=P)
    a_v = lora_a.rearrange("a (p c) r -> a p (c r)", c=C)
    w_v = weight.rearrange("(w p) h -> w p h", p=P)
    gate_v = gate_w.rearrange("e (p c) -> p e c", c=C)
    ics_v = ics.rearrange("e (p c) -> p e c", c=C)

    with ExitStack() as ctx:
        def sb(name, shape, dt):
            return ctx.enter_context(nc.sbuf_tensor(name, shape, dt))

        def ps(name, shape, dt):
            return ctx.enter_context(nc.psum_tensor(name, shape, dt))

        def sem(name):
            return ctx.enter_context(nc.semaphore(name))

        wt = sb("sign_w_T", [P, C, O], F16)
        xb = sb("x_rows", [P, 2, T, H], F32)
        bc = sb("bx_logit_weights", [P, C, NB, BW], F32)
        bcur = sb("bx_logit_weights_now", [P, 2, C, CT], F32)
        asel = sb("a_selected", [P, NB, C, R], F32)
        icss = sb("in_scale_scaled", [P, E, C], F32)
        icsb = sb("in_scale_entry", [P, E * C], F32)
        gate = sb("gate_cols", [P, E, C], F32)
        g = sb("g_parts", [P, 2, 2, C, RE], F16)
        gtmp = sb("g_full", [P, 2, CQ, RE], F32)
        m = sb("m_rows", [P, O], F32)
        xT = sb("x_T", [P, XTB, T, P], F32)
        biasb = sb("bias_rows", [P, O], F32)
        oparts = sb("out_scale_stack", [K2, O], BF16)
        pT = sb("p_T", [P, 2, T, P], F32)
        rT = sb("r_T", [K2, 2, T, P], BF16)
        work = sb("work", [P, (OSB + 2) * QW], F32)
        oscale = work[:, 0:OSB * QW].rearrange("p (n q) -> p n q", n=OSB)
        scaled = work[:, OSB * QW:(OSB + 2) * QW].rearrange("p (n q) -> p n q", n=2)
        sgn = work[:, 0:H].bitcast(F16).rearrange("p (n h) -> p n h", n=2)
        bsel = m
        acols = bc[:].rearrange("p c b w -> p (c b w)")[:, 0:C * P].rearrange("p (c n) -> p c n", c=C)
        ident = sb("ident", [P, P], F32)
        ident16 = sb("ident16", [P, P], F16)
        identb = sb("identb", [P, P], BF16)
        rw = sb("b_to_logits", [P, NB, E], F32)
        ga = sb("gate_a", [P, E], F32)
        diag = sb("batch_diag", [P, NB], F32)
        absmax = sb("absmax", [P, NB + 1], F32)
        allmax = sb("allmax", [P, NB + 1], F32)
        pow2 = sb("pow2", [P, NB + 1], F32)
        upscale = sb("upscale", [P, NB + 1], F32)
        unscale = sb("unscale", [P, NB], F32)
        unow = sb("unscale_now", [P, 2], F32)
        idrow = sb("id_row", [1, NB], I32)
        bxl = sb("bx_logits", [P, T, BW], F32)
        mx = sb("logit_max", [P, T], F32)
        ex = sb("exps", [P, T, E], F32)
        sm = sb("exp_sum", [P, T], F32)
        rs = sb("exp_sum_inv", [P, T], F32)
        rt = sb("routing", [P, T, E], F32)
        rd = sb("routing_rest", [P, T, E], F32)
        rparts = sb("routing_parts", [P, T, PARTS, PARTS, E], BF16)
        pn = sb("p_rows", [P, T, R, E], F32)
        ofull = biasb[0:E, :]
        op16 = [g[0:E, 1, 0].rearrange("p c n -> p (c n)").bitcast(BF16),
                g[0:E, 1, 1].rearrange("p c n -> p (c n)").bitcast(BF16),
                pT[0:E].rearrange("p a t n -> p (a t n)").bitcast(BF16)]
        accs = pn[:].rearrange("p t r e -> p (t r e)")
        fold = sb("tile_fold", [P, BW], F32)

        psM = ps("ps_m", [P, 2, QW], F32)
        psT = ps("ps_x_T", [P, 2, QW], F32)
        psPre = ps("ps_pre", [P, QW], F32)
        psOs = ps("ps_oscale", [P, QW], F32)
        psP = ps("ps_p_T", [P, T, P], F32)
        psS = ps("ps_small", [P, QW], F32)
        psA = psP[:].rearrange("p t n -> p (t n)")
        psB = [psM[:, 0], psM[:, 1], psT[:, 0], psT[:, 1]]
        acc = psS[:, 0:T * BW].rearrange("p (t w) -> p t w", t=T)
        psR = psS[:, QW // 2:QW].bitcast(BF16).rearrange("p (t n) -> p t n", t=T)
        psW = [psPre[:].bitcast(F16).rearrange("p (c n) -> p c n", c=HALF),
               psOs[:].bitcast(F16).rearrange("p (c n) -> p c n", c=HALF)]

        ids_in = sem("ids_in")
        gate_in = sem("gate_in")
        ics_in = sem("ics_in")
        bias_in = sem("bias_in")
        ocs_in = sem("ocs_in")
        a_in = sem("a_in")
        b_in = sem("b_in")
        w_in = [sem(f"w_in{i}") for i in range(4)]
        x_in = [[sem(f"x_in{i}_{q}") for q in range(Q)] for i in range(2)]
        stored = [[sem(f"stored{i}_{q}") for q in range(Q)] for i in range(2)]
        osplit = sem("osplit")
        ostack_in = sem("ostack_in")
        ident_ok = sem("ident_ok")
        opart_ok = sem("opart_ok")
        max_ok = sem("max_ok")
        allmax_ok = sem("allmax_ok")
        acols_ok = sem("acols_ok")
        bcur_zero = sem("bcur_zero")
        fold_ok = sem("fold_ok")
        ga_done = sem("ga_done")
        prep = sem("prep")
        rw_ok = sem("rw_ok")
        scale_ok = sem("scale_ok")
        ics_scaled = sem("ics_scaled")
        icsb_ok = sem("icsb_ok")
        bcmm_done = sem("bcmm_done")
        btr_done = sem("btr_done")
        bt_ok = sem("bt_ok")
        bc_ok = sem("bc_ok")
        sign_ok = sem("sign_ok")
        wtr_done = sem("wtr_done")
        wt_ok = sem("wt_ok")
        bcur_ok = sem("bcur_ok")
        gfull_ok = sem("gfull_ok")
        ghigh_ok = sem("ghigh_ok")
        glow_ok = sem("glow_ok")
        xtr_done = sem("xtr_done")
        xT_ok = sem("xT_ok")
        bx_done = sem("bx_done")
        acc_ok = sem("acc_ok")
        fold_done = sem("fold_done")
        m_done = sem("m_done")
        m_ok = sem("m_ok")
        chain = sem("chain")
        exp_in = sem("exp_in")
        exp_ok = sem("exp_ok")
        rp_ok = sem("rp_ok")
        pr_done = sem("pr_done")
        pT_ok = sem("pT_ok")
        rT_ok = sem("rT_ok")
        pre_done = sem("pre_done")
        os_done = sem("os_done")
        oscale_ok = sem("oscale_ok")
        mul_done = sem("mul_done")
        xbias_ok = sem("xbias_ok")
        out_ok = sem("out_ok")

        block = ctx.enter_context(nc.Block())

        UNITS = [[2 * s, 2 * s + 1] if 2 * s < C else [] for s in range(UN)]
        FOLD = C // 2
        SOFT = FOLD + 1
        PTR = SOFT + 3

        class Step:
            def __init__(self, j, par):
                self.j, self.par = j, par

            def at(self, per, c):
                if isinstance(self.j, int):
                    return per * (2 * self.j + self.par) + c
                return self.j * (2 * per) + (per * self.par + c)

            def half(self, per, c):
                return self.j * per + c

        def steps(eng, body):
            with eng.Fori(0, NB // 2 - 1) as j:
                body(Step(j, 0), True, True)
                body(Step(j, 1), True, True)
            body(Step(NB // 2 - 1, 0), True, False)
            body(Step(NB // 2 - 1, 1), False, False)

        @block.sync
        def _(sp):
            def load_x(b, par, q, who):
                return sp.dma_start(xb[:, par, :, q * QW:(q + 1) * QW],
                                    who[:, :, q * QW:(q + 1) * QW]).then_inc(x_in[par][q], 16)

            sp.dma_start(idrow[:], ids.rearrange("(a b) -> a b", a=1)).then_inc(ids_in, 16)
            sp.dma_start(icss[:], ics_v).then_inc(ics_in, 16)
            for w in range(WT):
                if w == 1:
                    sp.wait_ge(ids_in, 16)
                    for b in range(NB):
                        a = sp.value_load(idrow[0:1, b:b + 1], min_val=0, max_val=NA - 1)
                        sp.dma_start(asel[:, b].rearrange("p c r -> p (c r)"),
                                     a_v[bass.ds(a, 1)].rearrange("a p n -> (a p) n")).then_inc(a_in, 16)
                        sp.dma_start(bsel[b * R:(b + 1) * R, :],
                                     lora_b[bass.ds(a, 1)].rearrange("a r i -> (a r) i")).then_inc(b_in, 16)
                    sp.dma_start(gate[:], gate_v).then_inc(gate_in, 16)
                if w >= 4:
                    sp.wait_ge(sign_ok, w - 3)
                sp.dma_start(xb[:, 1, w % 4, :], w_v[w]).then_inc(w_in[w % 4], 16)
                if w % 4 == 1:
                    load_x(0, 0, w // 4, x_v[0])
                if w == 6:
                    sp.dma_start(ofull, ocs).then_inc(ocs_in, 16)
                if w == 10:
                    sp.wait_ge(opart_ok, 3)
                    for i in range(PARTS):
                        for jj in range(PARTS):
                            row = (i * PARTS + jj) * E
                            sp.dma_start(oparts[row:row + E, :], op16[jj]).then_inc(ostack_in, 16)
                    sp.dma_start(biasb[:], bias.rearrange("(a o) -> a o", a=1).broadcast_to([P, O])).then_inc(bias_in, 16)
            sp.wait_ge(sign_ok, WT)
            for q in range(Q):
                load_x(1, 1, q, x_v[1])

            def body(k, ahead, ahead2):
                b = k.at(1, 0)
                src_out = out_v[b] if isinstance(b, int) else out_v[bass.ds(b, 1)].rearrange("b p t h -> (b p) t h")

                def reload(q):
                    b2 = k.at(1, 2)
                    src = x_v[b2] if isinstance(b2, int) else x_v[bass.ds(b2, 1)].rearrange("b p t h -> (b p) t h")
                    sp.wait_ge(stored[k.par][q], k.half(16, 16))
                    load_x(b2, k.par, q, src)

                for q in range(Q):
                    sp.wait_ge(out_ok, k.at(UN, T * (q + 1)))
                    sp.dma_start(src_out[:, :, q * QW:(q + 1) * QW],
                                 xb[:, k.par, :, q * QW:(q + 1) * QW]).then_inc(stored[k.par][q], 16)
                    if ahead2 and q >= 1:
                        reload(q - 1)
                if ahead2:
                    reload(Q - 1)

            steps(sp, body)
            for par in range(2):
                for q in range(Q):
                    sp.wait_ge(stored[par][q], 16 * (NB // 2))


        @block.gpsimd
        def _(pool):
            nc.gpsimd.memset(ident[:], 0.0).then_inc(ident_ok, 1)
            pool.wait_ge(ident_ok, 1)
            nc.gpsimd.affine_select(out=ident[:], in_=ident[:], compare_op=ALU.not_equal, fill=1.0, base=0,
                                    pattern=[[-1, P]], channel_multiplier=1).then_inc(ident_ok, 1)
            pool.wait_ge(ident_ok, 2)
            nc.gpsimd.tensor_copy(ident16[:], ident[:]).then_inc(ident_ok, 1)
            nc.gpsimd.tensor_copy(identb[:], ident[:]).then_inc(ident_ok, 1)

            nc.gpsimd.memset(bcur[:], 0.0).then_inc(bcur_zero, 1)
            for jj in range(CQ):
                sl = slice(jj * CT, jj * CT + BW)
                if jj == 0:
                    nc.gpsimd.tensor_copy(fold[:], ident[:, sl]).then_inc(fold_ok, 1)
                else:
                    pool.wait_ge(fold_ok, jj)
                    nc.gpsimd.tensor_tensor(fold[:], fold[:], ident[:, sl], ALU.add).then_inc(fold_ok, 1)
            pool.wait_ge(max_ok, 2)
            nc.gpsimd.partition_all_reduce(allmax[:], absmax[:], P, bass.bass_isa.ReduceOp.max).then_inc(allmax_ok, 1)

            pool.wait_ge(scale_ok, 1)
            nc.gpsimd.tensor_tensor(icss[:], icss[:], upscale[:, NB:NB + 1].unsqueeze(2).broadcast_to([P, E, C]),
                                    ALU.mult).then_inc(ics_scaled, 1)
            pool.wait_ge(ics_scaled, 1)

            def scale_for(b, count, before):
                if before is not None:
                    pool.wait_ge(gfull_ok, before)
                u = upscale[:, b:b + 1] if isinstance(b, int) else upscale[:, bass.ds(b, 1)]
                nc.gpsimd.tensor_tensor(icsb[:], icss[:].rearrange("p e c -> p (e c)"), u.broadcast_to([P, E * C]),
                                        ALU.mult).then_inc(icsb_ok, 1)
                pool.wait_ge(icsb_ok, count)

            def g_full(b, par, grp, gate_count):
                a = asel[:, b] if isinstance(b, int) else asel[:, bass.ds(b, 1)].rearrange("p b c r -> p (b c) r")
                a = a[:, grp * CQ:(grp + 1) * CQ, :].unsqueeze(3).broadcast_to([P, CQ, R, E])
                for c in range(CQ):
                    cc = grp * CQ + c
                    i = nc.gpsimd.tensor_tensor(gtmp[:, grp % 2, c].rearrange("p (r e) -> p r e", e=E), a[:, c],
                                                icsb[:, cc:E * C:C].unsqueeze(1).broadcast_to([P, R, E]), ALU.mult)
                i.then_inc(gfull_ok, 1)

            def take_weights(b, par):
                src = bc[:, :, b, :] if isinstance(b, int) else bc[:, :, bass.ds(b, 1), :].rearrange("p c b w -> p c (b w)")
                nc.gpsimd.tensor_copy(bcur[:, par, :, 0:BW], src).then_inc(bcur_ok, 1)
                u = unscale[:, b:b + 1] if isinstance(b, int) else unscale[:, bass.ds(b, 1)]
                nc.gpsimd.tensor_copy(unow[:, par:par + 1], u).then_inc(bcur_ok, 1)

            for b in range(2):
                for grp in range(Q):
                    if b == 1 and grp == 0:
                        pool.wait_ge(ostack_in, 16 * K2 // E)
                    if grp == 0:
                        scale_for(b, b + 1, Q * b if b else None)
                    if 4 * b + grp >= 2:
                        pool.wait_ge(glow_ok, 4 * b + grp - 1)
                    g_full(b, b % 2, grp, None)
                    if 4 * b + grp == 1:
                        pool.wait_ge(bc_ok, 2)
                        take_weights(0, 0)
                        take_weights(1, 1)
            pool.wait_ge(bias_in, 16)

            def body(k, ahead, ahead2):
                if ahead2:
                    pool.wait_ge(bx_done, k.at(Q, Q))
                    pool.wait_ge(m_ok, k.at(Q, Q))
                    take_weights(k.at(1, 2), k.par)
                for s in range(UN):
                    q, t = divmod(s, T)
                    if s == 0:
                        pool.wait_ge(xtr_done, k.at(UN, UN))
                    xs = xb[:, k.par, t, q * QW:(q + 1) * QW]
                    nc.gpsimd.tensor_tensor(xs, xs, biasb[:, q * QW:(q + 1) * QW], ALU.add).then_inc(xbias_ok, 1)
                    if ahead2 and t == 1:
                        pool.wait_ge(glow_ok, k.at(Q, 2 * Q + q - 1))
                        if q == 0:
                            scale_for(k.at(1, 2), k.at(1, 3), k.at(Q, 2 * Q))
                        g_full(k.at(1, 2), k.par, q, None)

            steps(pool, body)

        @block.scalar
        def _(act):
            def g_high(par, grp):
                nc.scalar.activation(g[:, par, 0, grp * CQ:(grp + 1) * CQ, :], gtmp[:, grp % 2], ACT.Copy).then_inc(ghigh_ok, 1)

            def evac_x(u, count, tr, free):
                act.wait_ge(xtr_done, tr)
                if free is not None:
                    act.wait_ge(bx_done, free)
                nc.scalar.activation(xT[:, u % XTB], psT[:, u % 2, :].rearrange("p (t n) -> p t n", t=T), ACT.Copy).then_inc(xT_ok, 1)

            def evac_m(par, q, count, used):
                act.wait_ge(m_done, count)
                if used is not None:
                    act.wait_ge(pre_done, used)
                nc.scalar.activation(m[:, q * QW:(q + 1) * QW], psM[:, q % 2, :], ACT.Copy, scale=unow[:, par:par + 1]).then_inc(m_ok, 1)

            def exps(count):
                act.wait_ge(exp_in, count)
                nc.scalar.activation(ex[:], ex[:], ACT.Exp).then_inc(exp_ok, 1)

            def evac_r(par, count, used):
                act.wait_ge(pr_done, count)
                if used is not None:
                    act.wait_ge(os_done, used)
                nc.scalar.activation(rT[:, par], psR[0:K2], ACT.Copy).then_inc(rT_ok, 1)

            for w in range(WT):
                act.wait_ge(w_in[w % 4], 16 * (w // 4 + 1))
                if w >= 2:
                    act.wait_ge(wtr_done, 2 * (w - 1))
                nc.scalar.activation(sgn[:, w % 2, :], xb[:, 1, w % 4, :], ACT.Sign).then_inc(sign_ok, 1)
                if 3 <= w < 7 or w >= 8 and w < 12:
                    n = w - 3 if w < 7 else w - 4
                    act.wait_ge(gfull_ok, n + 1)
                    g_high(n // 4, n % 4)
                if w >= 3:
                    for u in range(3) if w == 3 else [w - 1]:
                        evac_x(u, None, u + 1, u // CQ if u >= XTB else None)
                if w >= 8 and w % 4 == 0:
                    if w == 8:
                        act.wait_ge(btr_done, Q)
                        act.wait_ge(bcur_ok, 4)
                    q = w // 4 - 2
                    evac_m(0, q, q + 1, None)
            evac_x(C - 1, None, C, Q - 1)
            evac_m(0, Q - 2, Q - 1, None)
            exps(1)
            evac_r(0, 1, None)
            evac_m(0, Q - 1, Q, None)

            def body(k, ahead, ahead2):
                for s in range(UN):
                    q, t = divmod(s, T)
                    act.wait_ge(os_done, k.at(UN, s + 1))
                    act.wait_ge(mul_done, k.at(UN, s + 1))
                    nc.scalar.activation(oscale[:, s % OSB, :], psOs[:], ACT.Copy).then_inc(oscale_ok, 1)
                    if ahead:
                        for u in UNITS[s]:
                            evac_x(u, None, k.at(C, C + u + 1), k.at(Q, Q + u // CQ))
                    if ahead2 and t == 2:
                        act.wait_ge(gfull_ok, k.at(Q, 2 * Q + q + 1))
                        if q == 0:
                            act.wait_ge(m_done, k.at(Q, Q))
                        g_high(k.par, q)
                    if ahead:
                        if s == SOFT:
                            exps(k.at(1, 2))
                        if s == PTR:
                            evac_r(1 - k.par, k.at(1, 2), k.at(UN, 1))
                        if t == 3:
                            evac_m(1 - k.par, q, k.at(Q, Q + q + 1), k.at(UN, s + 1))

            steps(act, body)

        @block.vector
        def _(dve):
            V = nc.vector
            def split_oscale():
                dve.wait_ge(ocs_in, 16)
                V.tensor_copy(op16[0], ofull).then_inc(opart_ok, 1)
                dve.wait_ge(opart_ok, 1)
                V.tensor_tensor(ofull, ofull, op16[0], ALU.subtract).then_inc(osplit, 1)
                dve.wait_ge(osplit, 1)
                V.tensor_copy(op16[1], ofull).then_inc(opart_ok, 1)
                dve.wait_ge(opart_ok, 2)
                V.tensor_tensor(op16[2], ofull, op16[1], ALU.subtract).then_inc(opart_ok, 1)

            def evac_w(w):
                for half in range(2):
                    dve.wait_ge(wtr_done, 2 * w + half + 1)
                    V.tensor_copy(wt[:, half * HALF:(half + 1) * HALF, w * P:(w + 1) * P], psW[half]).then_inc(wt_ok, 1)

            dve.wait_ge(ics_in, 16)
            V.tensor_reduce(absmax[:, NB:NB + 1], icss[:].rearrange("p e c -> p (e c)"), AX.X, ALU.max,
                            apply_absolute_value=True).then_inc(max_ok, 1)
            dve.wait_ge(a_in, 16 * NB)
            V.tensor_copy(acols.rearrange("p c (b r) -> p b c r", b=NB), asel[:]).then_inc(acols_ok, 1)
            V.tensor_reduce(absmax[:, 0:NB], asel[:].rearrange("p b c r -> p b (c r)"), AX.X, ALU.max,
                            apply_absolute_value=True).then_inc(max_ok, 1)
            dve.wait_ge(ident_ok, 4)
            V.tensor_reduce(diag[:], ident[:].rearrange("p (b r) -> p b r", r=R), AX.X, ALU.add).then_inc(prep, 1)
            dve.wait_ge(allmax_ok, 1)
            V.tensor_scalar(allmax[:], allmax[:], 2.0 ** -100, None, ALU.max).then_inc(prep, 1)
            dve.wait_ge(prep, 2)
            V.tensor_scalar(pow2[:].bitcast(I32), allmax[:].bitcast(I32), 0x7F800000, None,
                            ALU.bitwise_and).then_inc(prep, 1)
            dve.wait_ge(prep, 3)
            V.reciprocal(upscale[:], pow2[:]).then_inc(prep, 1)
            V.tensor_scalar(unscale[:], pow2[:, 0:NB], pow2[:, NB:NB + 1], 2.0 ** -13, ALU.mult, ALU.mult).then_inc(prep, 1)
            dve.wait_ge(prep, 4)
            V.tensor_scalar(upscale[:, 0:NB], upscale[:, 0:NB], 2.0 ** 7, None, ALU.mult).then_inc(prep, 1)
            V.tensor_scalar(upscale[:, NB:NB + 1], upscale[:, NB:NB + 1], 2.0 ** 6, None, ALU.mult).then_inc(scale_ok, 1)
            evac_w(0)
            dve.wait_ge(ga_done, 1)
            for n in range(Q):
                dve.wait_ge(btr_done, n + 1)
                V.tensor_copy(bc[:, n * CQ:(n + 1) * CQ, :, 0:R],
                              psB[n].rearrange("p (c b r) -> p c b r", c=CQ, b=NB)).then_inc(bt_ok, 1)
            V.tensor_copy(ga[:], psP[:, 0, 0:E]).then_inc(prep, 1)
            dve.wait_ge(prep, 7)
            V.tensor_tensor(rw[:], ga[:].unsqueeze(1).broadcast_to([P, NB, E]),
                            diag[:].unsqueeze(2).broadcast_to([P, NB, E]), ALU.mult).then_inc(rw_ok, 1)
            evac_w(1)
            for n in range(2):
                dve.wait_ge(bcmm_done, n + 1)
                V.tensor_copy(bc[:, n * HALF:(n + 1) * HALF, :, R:BW],
                              psM[:, n, :].rearrange("p (c b e) -> p c b e", c=HALF, b=NB)).then_inc(bc_ok, 1)

            def g_low(par, grp, count):
                dve.wait_ge(ghigh_ok, count)
                sl = slice(grp * CQ, (grp + 1) * CQ)
                V.tensor_tensor(g[:, par, 1, sl, :], gtmp[:, grp % 2], g[:, par, 0, sl, :], ALU.subtract).then_inc(glow_ok, 1)

            CH = 9

            def evac_acc(b, first):
                dve.wait_ge(bx_done, b(Q, Q))
                if not first:
                    dve.wait_ge(pr_done, b(1, 0))
                V.tensor_copy(accs, psA).then_inc(acc_ok, 1)

            def softmax(b, part):
                def link(i, c):
                    i.then_inc(chain, 1)
                    dve.wait_ge(chain, b(CH, c))

                if part == 0:
                    dve.wait_ge(fold_done, b(1, 1))
                    link(V.tensor_copy(bxl[:], acc), 1)
                    link(V.tensor_reduce(mx[:], bxl[:, :, R:BW], AX.X, ALU.max), 2)
                    V.tensor_tensor(ex[:], bxl[:, :, R:BW], mx[:].unsqueeze(2).broadcast_to([P, T, E]),
                                    ALU.subtract).then_inc(exp_in, 1)
                if part == 1:
                    dve.wait_ge(exp_ok, b(1, 1))
                    link(V.tensor_reduce(sm[:], ex[:], AX.X, ALU.add), 3)
                    link(V.reciprocal(rs[:], sm[:]), 4)
                    link(V.tensor_tensor(rt[:], ex[:], rs[:].unsqueeze(2).broadcast_to([P, T, E]), ALU.mult), 5)
                    V.tensor_tensor(pn[:], bxl[:, :, 0:R].unsqueeze(3).broadcast_to([P, T, R, E]),
                                    rt[:].unsqueeze(2).broadcast_to([P, T, R, E]), ALU.mult).then_inc(rp_ok, 1)
                if part == 2:
                    for i in range(PARTS):
                        src = rt if i == 0 else rd
                        for jj in range(PARTS):
                            ins = V.tensor_copy(rparts[:, :, i, jj, :], src[:])
                            if i == PARTS - 1:
                                if jj == PARTS - 1:
                                    ins.then_inc(rp_ok, 1)
                            elif jj == 0:
                                ins.then_inc(chain, 1)
                        if i < PARTS - 1:
                            dve.wait_ge(chain, b(CH, 6 + 2 * i))
                            link(V.tensor_tensor(rd[:], src[:], rparts[:, :, i, 0, :], ALU.subtract), 7 + 2 * i)

            def evac_p(par, count, used):
                dve.wait_ge(pr_done, count)
                if used is not None:
                    dve.wait_ge(pre_done, used)
                V.tensor_copy(pT[:, par], psP[:]).then_inc(pT_ok, 1)

            for w in range(2, WT):
                evac_w(w)
                if w == 5:
                    split_oscale()
                if 3 <= w < 7 or w >= 8 and w < 12:
                    n = w - 3 if w < 7 else w - 4
                    g_low(n // 4, n % 4, n + 1)
            fixed = lambda per, c: c
            evac_acc(fixed, True)
            softmax(fixed, 0)
            softmax(fixed, 1)
            softmax(fixed, 2)
            evac_p(0, 1, None)

            def body(k, ahead, ahead2):
                for s in range(UN):
                    q, t = divmod(s, T)
                    n = s % 2
                    if ahead and s == FOLD:
                        evac_acc(lambda per, c: k.at(per, per + c), False)
                    dve.wait_ge(pre_done, k.at(UN, s + 1))
                    dve.wait_ge(oscale_ok, k.at(UN, s + 1))
                    V.tensor_tensor(scaled[:, n], psPre[:], oscale[:, s % OSB], ALU.mult).then_inc(mul_done, 1)
                    dve.wait_ge(mul_done, k.at(UN, s + 3))
                    dve.wait_ge(xbias_ok, k.at(UN, s + 1))
                    xs = xb[:, k.par, t, q * QW:(q + 1) * QW]
                    V.tensor_tensor(xs, xs, scaled[:, n], ALU.add).then_inc(out_ok, 1)
                    if ahead2 and t == 3:
                        g_low(k.par, q, k.at(Q, 2 * Q + q + 1))
                    if ahead:
                        nxt = lambda per, c: k.at(per, per + c)
                        if SOFT <= s < SOFT + 3:
                            softmax(nxt, s - SOFT)
                        if s == PTR:
                            evac_p(1 - k.par, k.at(1, 2), k.at(UN, 1))

            for i in range(OSB):
                V.memset(mx[:, i:i + 1], 0.0).then_inc(mul_done, 1)
            steps(dve, body)

        @block.tensor
        def _(pe):
            mm = nc.tensor.matmul

            def transpose_x(u, par, loaded, free):
                if loaded is not None:
                    pe.wait_ge(x_in[par][u // CQ], loaded)
                if free is not None:
                    pe.wait_ge(xT_ok, free)
                for t in range(T):
                    i = nc.tensor.transpose(psT[:, u % 2, t * P:(t + 1) * P], xb[:, par, t, u * P:(u + 1) * P],
                                            ident[:])
                i.then_inc(xtr_done, 1)

            def product_x(grp, par, ready):
                pe.wait_ge(xT_ok, ready)
                for jj in range(CQ):
                    i = mm(psA[jj * CT:(jj + 1) * CT, :], bcur[:, par, grp * CQ + jj, :],
                           xT[:, jj].rearrange("p t n -> p (t n)"), start=(grp == 0), stop=(grp == Q - 1))
                i.then_inc(bx_done, 1)

            def fold_tiles(ready, free):
                if free is not None:
                    pe.wait_ge(rT_ok, free)
                pe.wait_ge(acc_ok, ready)
                for t in range(T):
                    i = mm(acc[:, t, :], accs[:, t * P:(t + 1) * P], fold[:], start=True, stop=True)
                i.then_inc(fold_done, 1)

            def product_m(q, t, par, free):
                if t == 0 and free is not None:
                    pe.wait_ge(m_ok, free)
                for c in range(t * CQ, (t + 1) * CQ):
                    for part in range(2):
                        i = mm(psM[:, q % 2, :], g[:, par, part, c, :], wt[:, c, q * QW:(q + 1) * QW],
                               start=(c == 0 and part == 0), stop=(c == C - 1 and part == 1))
                if t == T - 1:
                    i.then_inc(m_done, 1)

            def transpose_pr(ready):
                pe.wait_ge(rp_ok, ready)
                for t in range(T):
                    nc.tensor.transpose(psP[:, t, :], pn[:, t].rearrange("p r e -> p (r e)"), ident[:])
                for t in range(T):
                    i = nc.tensor.transpose(psR[0:K2, t, :], rparts[:, t].rearrange("p i j e -> p (i j e)"), identb[:])
                i.then_inc(pr_done, 1)

            def transpose_w(w):
                pe.wait_ge(sign_ok, w + 1)
                for half in range(2):
                    if w >= 1:
                        pe.wait_ge(wt_ok, 2 * (w - 1) + half + 1)
                    for c in range(HALF):
                        i = nc.tensor.transpose(psW[half][:, c, :],
                                                sgn[:, w % 2, half * HALF + c:H:C], ident16[:])
                    i.then_inc(wtr_done, 1)

            pe.wait_ge(ident_ok, 4)
            transpose_w(0)
            pe.wait_ge(gate_in, 16)
            pe.wait_ge(acols_ok, 1)
            for c in range(C):
                i = mm(psP[:, 0, 0:E], acols[:, c, :], gate[:, :, c], start=(c == 0), stop=(c == C - 1))
            i.then_inc(ga_done, 1)
            pe.wait_ge(b_in, 16 * NB)
            for c in range(C):
                i = nc.tensor.transpose(psB[c // CQ][:, (c % CQ) * P:(c % CQ + 1) * P], bsel[:, c * P:(c + 1) * P],
                                        ident[:])
                if c % CQ == CQ - 1:
                    i.then_inc(btr_done, 1)
            transpose_w(1)
            pe.wait_ge(rw_ok, 1)
            pe.wait_ge(bt_ok, Q)
            for c in range(C):
                i = mm(psM[:, c // HALF, (c % HALF) * NB * E:(c % HALF + 1) * NB * E], bsel[:, c * P:(c + 1) * P],
                       rw[:].rearrange("p b e -> p (b e)"), start=True, stop=True)
                if c % HALF == HALF - 1:
                    i.then_inc(bcmm_done, 1)
            transpose_w(2)
            transpose_x(0, 0, 16, None)
            transpose_x(1, 0, None, None)
            for w in range(3, WT + 4):
                if w <= WT:
                    u = w - 1
                    transpose_x(u, 0, 16 if u % CQ == 0 else None, u - 1)
                if w < WT:
                    transpose_w(w)
                if w >= 4:
                    q, t = divmod(w - 4, T)
                    if t == 0:
                        pe.wait_ge(wt_ok, 2 * w)
                        if q == 0:
                            pe.wait_ge(bc_ok, 2)
                    if q == 0:
                        pe.wait_ge(glow_ok, t + 1)
                    if w == WT + 3:
                        transpose_pr(2)
                    product_m(q, t, 0, q - 1 if q >= 2 else None)
                if w <= WT and w % CQ == 0:
                    if w == CQ:
                        pe.wait_ge(bcur_ok, 2)
                        pe.wait_ge(fold_ok, CQ)
                    product_x(w // CQ - 1, 0, w)
                if w == WT + 1:
                    fold_tiles(1, None)

            def body(k, ahead, ahead2):
                for s in range(UN):
                    q, t = divmod(s, T)
                    sl = slice(q * QW, (q + 1) * QW)
                    if s == 0:
                        pe.wait_ge(pT_ok, k.at(1, 1))
                    if t == 0:
                        pe.wait_ge(m_ok, k.at(Q, q + 1))
                    pe.wait_ge(mul_done, k.at(UN, s + 2))
                    mm(psPre[:], pT[:, k.par, t, :], m[:, sl], start=True, stop=True).then_inc(pre_done, 1)
                    if s == 0:
                        pe.wait_ge(rT_ok, k.at(1, 1))
                    mm(psOs[:], rT[:, k.par, t, :], oparts[:, sl], start=True, stop=True).then_inc(os_done, 1)
                    if ahead:
                        for u in UNITS[s]:
                            transpose_x(u, 1 - k.par,
                                        k.half(16, 16 + 16 * k.par) if u % CQ == 0 else None,
                                        k.at(C, C + u - 1))
                        if s == 0:
                            pe.wait_ge(glow_ok, k.at(Q, 2 * Q))
                            pe.wait_ge(bcur_ok, k.at(2, 4))
                        if s == FOLD:
                            fold_tiles(k.at(1, 2), None)
                        product_m(q, t, 1 - k.par, k.at(Q, Q + q - 1))
                        for u in UNITS[s]:
                            if u % CQ == CQ - 1:
                                product_x(u // CQ, 1 - k.par, k.at(C, C + u + 1))
                        if s == PTR:
                            transpose_pr(k.at(2, 4))

            pe.wait_ge(ostack_in, 16 * K2 // E)
            steps(pe, body)


_INS = ['x', 'itok_B_3_7', 'L0_cond_A', 'L0_cond_B', 'L0_ffn_weight', 'L0_ffn_bias', 'L0_ffn_gate_w',
        'L0_ffn_in_channel_scale', 'L0_ffn_out_channel_scale']


def kernel(**inputs):
    import numpy as _np
    import concourse.bacc as _bacc
    from concourse import mybir as _mybir
    from concourse.bass_utils import run_bass_kernel_spmd as _run

    nc = _bacc.Bacc("TRN2", target_bir_lowering=False, num_devices=1, dynamic_dma_scratch_size=1024)
    arrays, args = {}, []
    for name in _INS:
        a = _np.ascontiguousarray(inputs[name])
        arrays[f"in_{name}_dram"] = a
        args.append(nc.dram_tensor(f"in_{name}_dram", a.shape, _mybir.dt.from_np(a.dtype), kind="ExternalInput").ap())
    shape = inputs['x'].shape
    args.append(nc.dram_tensor("out_0_dram", shape, _mybir.dt.float32, kind="ExternalOutput").ap())
    adaln_ffn(nc, *args)
    r = _run(nc, [arrays], core_ids=[0])
    return r.results[0]["out_0_dram"]
```

```python
from contextlib import ExitStack

import concourse.bass as bass
from concourse import mybir


P = 128
F32 = mybir.dt.float32
F16 = mybir.dt.float16
BF16 = mybir.dt.bfloat16
I32 = mybir.dt.int32
ALU = mybir.AluOpType
ACT = mybir.ActivationFunctionType
AX = mybir.AxisListType


def adaln_ffn(nc, x, ids, lora_a, lora_b, weight, bias, gate_w, ics, ocs, out):
    NB, S, H = x.shape
    NA, O, R = lora_a.shape
    E = gate_w.shape[0]
    C = H // P
    T = S // P
    QW = 512
    Q = O // QW
    CQ = C // Q
    RE = R * E
    BW = R + E
    CT = 32
    PARTS = 3
    K2 = PARTS * PARTS * E
    UN = Q * T
    WT = O // P
    HALF = C // 2
    OSB = 4
    XTB = 4
    assert CQ * CT == P and BW <= CT and XTB == CQ
    assert RE == P and NB * R == P and H == O and Q * CQ == C and CQ == T == 4 and NB == 8

    x_v = x.rearrange("b (t p) h -> b p t h", p=P)
    out_v = out.rearrange("b (t p) h -> b p t h", p=P)
    a_v = lora_a.rearrange("a (p c) r -> a p (c r)", c=C)
    w_v = weight.rearrange("(w p) h -> w p h", p=P)
    gate_v = gate_w.rearrange("e (p c) -> p e c", c=C)
    ics_v = ics.rearrange("e (p c) -> p e c", c=C)

    with ExitStack() as ctx:
        def sb(name, shape, dt):
            return ctx.enter_context(nc.sbuf_tensor(name, shape, dt))

        def ps(name, shape, dt):
            return ctx.enter_context(nc.psum_tensor(name, shape, dt))

        def sem(name):
            return ctx.enter_context(nc.semaphore(name))

        wt = sb("sign_w_T", [P, C, O], F16)
        xb = sb("x_rows", [P, 2, T, H], F32)
        bc = sb("bx_logit_weights", [P, C, NB, BW], F32)
        bcur = sb("bx_logit_weights_now", [P, 2, C, CT], F32)
        asel = sb("a_selected", [P, NB, C, R], F32)
        icss = sb("in_scale_scaled", [P, E, C], F32)
        icsb = sb("in_scale_entry", [P, E * C], F32)
        gate = sb("gate_cols", [P, E, C], F32)
        g = sb("g_parts", [P, 2, 2, C, RE], F16)
        gtmp = sb("g_full", [P, 2, CQ, RE], F32)
        m = sb("m_rows", [P, O], F32)
        xT = sb("x_T", [P, XTB, T, P], F32)
        biasb = sb("bias_rows", [P, O], F32)
        oparts = sb("out_scale_stack", [K2, O], BF16)
        pT = sb("p_T", [P, 2, T, P], F32)
        rT = sb("r_T", [K2, 2, T, P], BF16)
        scaled = sb("scaled", [P, OSB, QW], F32)
        sgn = scaled[:].rearrange("p n q -> p (n q)")[:, 0:H].bitcast(F16).rearrange("p (n h) -> p n h", n=2)
        bsel = m
        acols = bc[:].rearrange("p c b w -> p (c b w)")[:, 0:C * P].rearrange("p (c n) -> p c n", c=C)
        ident = sb("ident", [P, P], F32)
        ident16 = sb("ident16", [P, P], F16)
        identb = sb("identb", [P, P], BF16)
        rw = sb("b_to_logits", [P, NB, E], F32)
        ga = sb("gate_a", [P, E], F32)
        diag = sb("batch_diag", [P, NB], F32)
        absmax = sb("absmax", [P, NB + 1], F32)
        allmax = sb("allmax", [P, NB + 1], F32)
        pow2 = sb("pow2", [P, NB + 1], F32)
        upscale = sb("upscale", [P, NB + 1], F32)
        unscale = sb("unscale", [P, NB], F32)
        unow = sb("unscale_now", [P, 2], F32)
        idrow = sb("id_row", [1, NB], I32)
        number = sb("number", [1, NB], I32)
        numberf = sb("number_f", [1, NB], F32)
        idf = sb("id_f", [1, NB], F32)
        key = sb("key", [1, NB], F32)
        pairs = sb("pairs", [1, 3, NB, NB], F32)
        rank = sb("rank", [1, NB], F32)
        sortedf = sb("sorted_f", [1, 2, NB], F32)
        order = sb("order", [1, NB], I32)
        adapter = sb("adapter", [1, NB], I32)
        isnew = sb("is_new", [1, NB], I32)
        mx = sb("logit_max", [P, T], F32)
        ex = sb("exps", [P, T, E], F32)
        sm = sb("exp_sum", [P, T], F32)
        rs = sb("exp_sum_inv", [P, T], F32)
        rt = sb("routing", [P, T, E], F32)
        rd = sb("routing_rest", [P, T, E], F32)
        rparts = sb("routing_parts", [P, T, PARTS, PARTS, E], BF16)
        pn = sb("p_rows", [P, T, R, E], F32)
        ofull = pT[:, 0, 0, :]
        op16 = [pT[:, 0, 1 + i, 0:P // 2].bitcast(BF16) for i in range(PARTS)]
        accs = pn[:].rearrange("p t r e -> p (t r e)")
        fold = sb("tile_fold", [P, BW], F32)

        psM = ps("ps_m", [P, 2, QW], F32)
        psT = ps("ps_x_T", [P, 2, QW], F32)
        psPre = ps("ps_pre", [P, 2, QW], F32)
        psOs = ps("ps_oscale", [P, QW], F32)
        psP = ps("ps_p_T", [P, T, P], F32)
        psA = psP[:].rearrange("p t n -> p (t n)")
        psB = [psM[:, 0], psM[:, 1], psT[:, 0], psT[:, 1]]
        acc = psA[:, 0:T * BW].rearrange("p (t w) -> p t w", t=T)
        psR = psT[:, 0, 0:QW // 2].bitcast(BF16).rearrange("p (t n) -> p t n", t=T)
        psR0 = psOs[:, 0:QW // 2].bitcast(BF16).rearrange("p (t n) -> p t n", t=T)
        psW = [psPre[:, 0].bitcast(F16).rearrange("p (c n) -> p c n", c=HALF),
               psOs[:].bitcast(F16).rearrange("p (c n) -> p c n", c=HALF)]

        ids_in = sem("ids_in")
        number_ok = sem("number_ok")
        sort_step = sem("sort_step")
        order_ok = sem("order_ok")
        gate_in = sem("gate_in")
        ics_in = sem("ics_in")
        bias_in = sem("bias_in")
        ocs_in = sem("ocs_in")
        a_in = sem("a_in")
        b_in = sem("b_in")
        w_in = [sem(f"w_in{i}") for i in range(4)]
        x_in = [[sem(f"x_in{i}_{q}") for q in range(Q)] for i in range(2)]
        stored = [[sem(f"stored{i}_{q}") for q in range(Q)] for i in range(2)]
        osplit = sem("osplit")
        ostack_in = sem("ostack_in")
        ident_ok = sem("ident_ok")
        opart_ok = sem("opart_ok")
        max_ok = sem("max_ok")
        allmax_ok = sem("allmax_ok")
        acols_ok = sem("acols_ok")
        bcur_zero = sem("bcur_zero")
        fold_ok = sem("fold_ok")
        gcols_ok = sem("gcols_ok")
        gtiles_done = sem("gtiles_done")
        gtiles_ok = sem("gtiles_ok")
        ga_done = sem("ga_done")
        prep = sem("prep")
        rw_ok = sem("rw_ok")
        scale_ok = sem("scale_ok")
        ics_scaled = sem("ics_scaled")
        icsb_ok = sem("icsb_ok")
        bcmm_done = sem("bcmm_done")
        btr_done = sem("btr_done")
        bt_ok = sem("bt_ok")
        bc_ok = sem("bc_ok")
        sign_ok = sem("sign_ok")
        wtr_done = sem("wtr_done")
        wt_ok = sem("wt_ok")
        bcur_ok = sem("bcur_ok")
        gfull_ok = sem("gfull_ok")
        ghigh_ok = sem("ghigh_ok")
        glow_ok = sem("glow_ok")
        xtr_done = sem("xtr_done")
        xT_ok = sem("xT_ok")
        bx_done = sem("bx_done")
        acc_ok = sem("acc_ok")
        fold_done = sem("fold_done")
        m_done = sem("m_done")
        m_ok = sem("m_ok")
        chain = sem("chain")
        exp_in = sem("exp_in")
        exp_ok = sem("exp_ok")
        rp_ok = sem("rp_ok")
        pr_done = sem("pr_done")
        pT_ok = sem("pT_ok")
        rT_ok = sem("rT_ok")
        pre_done = sem("pre_done")
        os_done = sem("os_done")
        oscale_ok = sem("oscale_ok")
        mul_done = sem("mul_done")
        xbias_ok = sem("xbias_ok")
        out_ok = sem("out_ok")
        pool_out_ok = sem("pool_out_ok")

        block = ctx.enter_context(nc.Block())

        FIRST = {1: 5, 2: 7, 3: 8, 4: 10, 5: 11, 6: 12, 7: 14, 8: 15, 11: 16, 12: 17, 13: 18, 14: 19}
        SECOND = {0: 4, 1: 6, 3: 9, 6: 13}
        assert sorted([*FIRST.values(), *SECOND.values()]) == list(range(CQ, C + CQ))
        GROUP = {1: 0, 3: 1, 6: 2, 9: 3}
        FOLD = 9
        TAKE = FOLD + 1
        PTR = UN - 1
        GSLOT = {1: 0, 3: 1, 5: 2, 7: 3}
        SOFT = {FOLD: ([], [0]), FOLD + 1: ([1], []), FOLD + 2: ([2], [3]), FOLD + 3: ([4], [5, 6, 7]), FOLD + 4: ([8], [9, 10])}

        POOL_T = 2

        def dve_tiles(s):
            return sum(i % T != POOL_T for i in range(s + 1))

        def unit(table, s, ahead, ahead2):
            u = table.get(s)
            return None if u is None or not (ahead if u < C else ahead2) else u

        class Step:
            def __init__(self, j, par):
                self.j, self.par = j, par

            def at(self, per, c):
                if isinstance(self.j, int):
                    return per * (2 * self.j + self.par) + c
                return self.j * (2 * per) + (per * self.par + c)

            def half(self, per, c):
                return self.j * per + c

        def steps(eng, body):
            with eng.Fori(0, NB // 2 - 1) as j:
                body(Step(j, 0), True, True)
                body(Step(j, 1), True, True)
            body(Step(NB // 2 - 1, 0), True, False)
            body(Step(NB // 2 - 1, 1), False, False)

        @block.sync
        def _(sp):
            def entry(dram, k):
                at = order[0:1, k:k + 1] if isinstance(k, int) else order[0:1, bass.ds(k, 1)]
                b = sp.value_load(at, min_val=0, max_val=NB - 1)
                return dram[bass.ds(b, 1)].rearrange("b p t h -> (b p) t h")

            def load_x(src, par, q):
                sp.dma_start(xb[:, par, :, q * QW:(q + 1) * QW],
                             src[:, :, q * QW:(q + 1) * QW]).then_inc(x_in[par][q], 16)

            sp.dma_start(idrow[:], ids.rearrange("(a b) -> a b", a=1)).then_inc(ids_in, 16)
            for w in range(WT):
                if w >= 4:
                    sp.wait_ge(sign_ok, w - 3)
                sp.dma_start(xb[:, 1, w % 4, :], w_v[w]).then_inc(w_in[w % 4], 16)
                if w == 0:
                    sp.dma_start(icss[:], ics_v).then_inc(ics_in, 16)
                    sp.dma_start(gate[:], gate_v).then_inc(gate_in, 16)
                    sp.dma_start(ofull, ocs.rearrange("e (j n) -> (e j) n", n=P)).then_inc(ocs_in, 16)
                if w == 2:
                    sp.wait_ge(order_ok, 3)
                    for b in range(NB):
                        a = sp.value_load(adapter[0:1, b:b + 1], min_val=0, max_val=NA - 1)
                        sp.dma_start(asel[:, b].rearrange("p c r -> p (c r)"),
                                     a_v[bass.ds(a, 1)].rearrange("a p n -> (a p) n")).then_inc(a_in, 16)
                        sp.dma_start(bsel[b * R:(b + 1) * R, :],
                                     lora_b[bass.ds(a, 1)].rearrange("a r i -> (a r) i")).then_inc(b_in, 16)
                    first = entry(x_v, 0)
                if w >= 3 and w % 3 == 0 and w // 3 <= Q:
                    load_x(first, 0, w // 3 - 1)
            sp.dma_start(biasb[:], bias.rearrange("(a o) -> a o", a=1).broadcast_to([P, O])).then_inc(bias_in, 16)
            sp.wait_ge(opart_ok, 3)
            for i in range(PARTS):
                for jj in range(PARTS):
                    row = (i * PARTS + jj) * E
                    sp.dma_start(oparts[row:row + E, :].rearrange("e (j n) -> e j n", n=P),
                                 op16[jj]).then_inc(ostack_in, 16)
            sp.wait_ge(sign_ok, WT)
            second = entry(x_v, 1)
            for q in range(Q):
                load_x(second, 1, q)

            def last_block(k, here, q):
                for t in range(T):
                    if q == Q - 1 or t == T - 1:
                        sp.wait_ge(out_ok, k.at(UN, OSB + dve_tiles(T * q + t)))
                        if t >= POOL_T:
                            sp.wait_ge(pool_out_ok, q + 1)
                    if q == Q - 1:
                        sp.dma_start(here[:, t:t + 1, q * QW:(q + 1) * QW],
                                     xb[:, k.par, t:t + 1, q * QW:(q + 1) * QW]).then_inc(stored[k.par][q], 16)
                if q < Q - 1:
                    sp.dma_start(here[:, :, q * QW:(q + 1) * QW],
                                 xb[:, k.par, :, q * QW:(q + 1) * QW]).then_inc(stored[k.par][q], 16)

            def body(k, ahead, ahead2):
                here = entry(out_v, k.at(1, 0))
                after = entry(x_v, k.at(1, 2)) if ahead2 else None

                for q in range(Q):
                    if not ahead:
                        last_block(k, here, q)
                        continue
                    sp.wait_ge(out_ok, k.at(UN, OSB + T * (q + 1)))
                    sp.dma_start(here[:, :, q * QW:(q + 1) * QW],
                                 xb[:, k.par, :, q * QW:(q + 1) * QW]).then_inc(stored[k.par][q], 16)
                    if ahead2:
                        sp.wait_ge(stored[k.par][q], k.half(16, 16))
                        load_x(after, k.par, q)

            steps(sp, body)
            for par in range(2):
                for q in range(Q):
                    split = par == 1 and q == Q - 1
                    sp.wait_ge(stored[par][q], 16 * (NB // 2 + (T - 1 if split else 0)))


        @block.gpsimd
        def _(pool):
            nc.gpsimd.memset(ident[:], 0.0).then_inc(ident_ok, 1)
            pool.wait_ge(ident_ok, 1)
            nc.gpsimd.affine_select(out=ident[:], in_=ident[:], compare_op=ALU.not_equal, fill=1.0, base=0,
                                    pattern=[[-1, P]], channel_multiplier=1).then_inc(ident_ok, 1)
            pool.wait_ge(ident_ok, 2)
            nc.gpsimd.tensor_copy(ident16[:], ident[:]).then_inc(ident_ok, 1)
            nc.gpsimd.tensor_copy(identb[:], ident[:]).then_inc(ident_ok, 1)

            nc.gpsimd.iota(number[:], pattern=[[1, NB]], base=0, channel_multiplier=0).then_inc(number_ok, 1)
            nc.gpsimd.memset(bcur[:], 0.0).then_inc(bcur_zero, 1)
            for jj in range(CQ):
                sl = slice(jj * CT, jj * CT + BW)
                if jj == 0:
                    nc.gpsimd.tensor_copy(fold[:], ident[:, sl]).then_inc(fold_ok, 1)
                else:
                    pool.wait_ge(fold_ok, jj)
                    nc.gpsimd.tensor_tensor(fold[:], fold[:], ident[:, sl], ALU.add).then_inc(fold_ok, 1)
            pool.wait_ge(gate_in, 16)
            pool.wait_ge(bcur_zero, 1)
            nc.gpsimd.tensor_copy(bcur[:, 0, :, 0:E], gate[:].rearrange("p e c -> p c e")).then_inc(gcols_ok, 1)
            pool.wait_ge(max_ok, 2)
            nc.gpsimd.partition_all_reduce(allmax[:], absmax[:], P, bass.bass_isa.ReduceOp.max).then_inc(allmax_ok, 1)

            pool.wait_ge(scale_ok, 1)
            nc.gpsimd.tensor_tensor(icss[:], icss[:], upscale[:, NB:NB + 1].unsqueeze(2).broadcast_to([P, E, C]),
                                    ALU.mult).then_inc(ics_scaled, 1)
            pool.wait_ge(ics_scaled, 1)

            def scale_for(b, count, before):
                if before is not None:
                    pool.wait_ge(gfull_ok, before)
                u = upscale[:, b:b + 1] if isinstance(b, int) else upscale[:, bass.ds(b, 1)]
                nc.gpsimd.tensor_tensor(icsb[:], icss[:].rearrange("p e c -> p (e c)"), u.broadcast_to([P, E * C]),
                                        ALU.mult).then_inc(icsb_ok, 1)
                pool.wait_ge(icsb_ok, count)

            def g_full(b, grp):
                a = asel[:, b] if isinstance(b, int) else asel[:, bass.ds(b, 1)].rearrange("p b c r -> p (b c) r")
                a = a[:, grp * CQ:(grp + 1) * CQ, :].unsqueeze(3).broadcast_to([P, CQ, R, E])
                i = nc.gpsimd.tensor_tensor(gtmp[:, grp % 2].rearrange("p c (r e) -> p c r e", e=E), a,
                                            icsb[:].rearrange("p (e c) -> p c e", e=E)[:, grp * CQ:(grp + 1) * CQ]
                                            .unsqueeze(2).broadcast_to([P, CQ, R, E]), ALU.mult)
                i.then_inc(gfull_ok, 1)

            def take_weights(b, par):
                src = bc[:, :, b, :] if isinstance(b, int) else bc[:, :, bass.ds(b, 1), :].rearrange("p c b w -> p c (b w)")
                nc.gpsimd.tensor_copy(bcur[:, par, :, 0:BW], src).then_inc(bcur_ok, 1)
                u = unscale[:, b:b + 1] if isinstance(b, int) else unscale[:, bass.ds(b, 1)]
                nc.gpsimd.tensor_copy(unow[:, par:par + 1], u).then_inc(bcur_ok, 1)

            for b in range(2):
                for grp in range(Q):
                    if grp == 0:
                        scale_for(b, b + 1, Q * b if b else None)
                    if 4 * b + grp >= 2:
                        pool.wait_ge(glow_ok, 4 * b + grp - 1)
                    g_full(b, grp)
                    if 4 * b + grp == 1:
                        pool.wait_ge(bc_ok, 2)
                        take_weights(0, 0)
                        take_weights(1, 1)
            pool.wait_ge(bias_in, 16)

            def body(k, ahead, ahead2):
                for s in range(UN):
                    q, t = divmod(s, T)
                    if s == 0:
                        pool.wait_ge(xtr_done, k.at(UN, UN))
                    xs = xb[:, k.par, t, q * QW:(q + 1) * QW]
                    nc.gpsimd.tensor_tensor(xs, xs, biasb[:, q * QW:(q + 1) * QW], ALU.add).then_inc(xbias_ok, 1)
                    if ahead2 and s == TAKE:
                        pool.wait_ge(oscale_ok, k.at(UN, 2))
                        take_weights(k.at(1, 2), k.par)
                    if ahead2 and s in GSLOT:
                        grp = GSLOT[s]
                        pool.wait_ge(glow_ok, k.at(Q, 2 * Q + grp - 1))
                        if grp == 0:
                            scale_for(k.at(1, 2), k.at(1, 3), k.at(Q, 2 * Q))
                        g_full(k.at(1, 2), grp)
                if not ahead:
                    pool.wait_ge(xbias_ok, k.at(UN, UN))
                    for q in range(Q):
                        s = T * q + POOL_T
                        pool.wait_ge(mul_done, k.at(UN, s + 3))
                        xs = xb[:, k.par, POOL_T, q * QW:(q + 1) * QW]
                        nc.gpsimd.tensor_tensor(xs, xs, scaled[:, s % OSB], ALU.add).then_inc(pool_out_ok, 1)

            steps(pool, body)

        @block.scalar
        def _(act):
            def g_high(par, grp):
                nc.scalar.activation(g[:, par, 0, grp * CQ:(grp + 1) * CQ, :], gtmp[:, grp % 2], ACT.Copy).then_inc(ghigh_ok, 1)

            def evac_x(u, count, tr, free):
                act.wait_ge(xtr_done, tr)
                if free is not None:
                    act.wait_ge(bx_done, free)
                nc.scalar.activation(xT[:, u % XTB], psT[:, u % 2, :].rearrange("p (t n) -> p t n", t=T), ACT.Copy).then_inc(xT_ok, 1)

            def evac_m(par, q):
                return nc.scalar.activation(m[:, q * QW:(q + 1) * QW], psM[:, q % 2, :], ACT.Copy, scale=unow[:, par:par + 1])

            def exps(count):
                act.wait_ge(exp_in, count)
                nc.scalar.activation(ex[:], ex[:], ACT.Exp).then_inc(exp_ok, 1)

            def evac_acc(count):
                act.wait_ge(bx_done, count)
                nc.scalar.activation(accs, psA, ACT.Copy).then_inc(acc_ok, 1)

            def evac_pr(par, count, psR=psR):
                act.wait_ge(pr_done, count)
                nc.scalar.activation(pT[:, par], psP[:], ACT.Copy).then_inc(pT_ok, 1)
                nc.scalar.activation(rT[:, par], psR[0:K2], ACT.Copy).then_inc(rT_ok, 1)

            for w in range(WT):
                act.wait_ge(w_in[w % 4], 16 * (w // 4 + 1))
                if w >= 2:
                    act.wait_ge(wtr_done, 2 * (w - 1))
                nc.scalar.activation(sgn[:, w % 2, :], xb[:, 1, w % 4, :], ACT.Sign).then_inc(sign_ok, 1)
                if 3 <= w < 7 or w >= 8 and w < 12:
                    n = w - 3 if w < 7 else w - 4
                    act.wait_ge(gfull_ok, n + 1)
                    g_high(n // 4, n % 4)
                if w >= 4:
                    for u in range(4) if w == 4 else [w - 1]:
                        evac_x(u, None, u + 1, u // CQ if u >= XTB else None)
                if w >= 8 and w % 4 == 0:
                    if w == 8:
                        act.wait_ge(btr_done, Q)
                        act.wait_ge(bcur_ok, 4)
                    q = w // 4 - 2
                    act.wait_ge(m_done, q + 1)
                    evac_m(0, q).then_inc(m_ok, 1)
            evac_x(C - 1, None, C, Q - 1)
            evac_acc(Q)
            act.wait_ge(m_done, Q - 1)
            evac_m(0, Q - 2).then_inc(m_ok, 1)
            exps(1)
            act.wait_ge(m_done, Q)
            evac_m(0, Q - 1).then_inc(m_ok, 1)
            act.wait_ge(ostack_in, 16 * K2 // E)
            evac_pr(0, 1, psR0)
            for u in range(C, C + CQ):
                evac_x(u, None, u + 1, Q)

            def body(k, ahead, ahead2):
                if ahead:
                    k1 = k.at(1, 1)
                    at = isnew[0:1, k1:k1 + 1] if isinstance(k1, int) else isnew[0:1, bass.ds(k1, 1)]
                    new = act.value_load(at, min_val=0, max_val=1)
                for s in range(UN):
                    q, t = divmod(s, T)
                    if ahead and s == FOLD:
                        evac_acc(k.at(Q, 2 * Q))
                    if ahead and s == FOLD + 2:
                        exps(k.at(1, 2))
                    u = unit(FIRST, s, ahead, ahead2)
                    if u is not None:
                        evac_x(u, None, k.at(C, C + u + 1), k.at(Q, Q + u // CQ))
                    if ahead and s == PTR:
                        evac_pr(1 - k.par, k.at(1, 2))
                    act.wait_ge(os_done, k.at(UN, s + 1))
                    if ahead or s < OSB:
                        act.wait_ge(out_ok, k.at(UN, s + 1))
                    elif t == POOL_T:
                        act.wait_ge(pool_out_ok, q)
                    else:
                        act.wait_ge(out_ok, k.at(UN, OSB + dve_tiles(s - OSB)))
                    nc.scalar.activation(scaled[:, s % OSB, :], psOs[:], ACT.Copy).then_inc(oscale_ok, 1)
                    u = unit(SECOND, s, ahead, ahead2)
                    if u is not None:
                        evac_x(u, None, k.at(C, C + u + 1), k.at(Q, Q + u // CQ))
                    if ahead2 and s - 1 in GSLOT:
                        grp = GSLOT[s - 1]
                        act.wait_ge(gfull_ok, k.at(Q, 2 * Q + grp + 1))
                        g_high(k.par, grp)
                    if ahead:
                        if q >= 1 and t == 0 or s == UN - 1:
                            with act.If(new == 1):
                                act.wait_ge(pre_done, k.at(UN, s + 1))
                                for qq in ([q - 1] if t == 0 else [Q - 1]):
                                    evac_m(1 - k.par, qq)

            act.wait_ge(order_ok, 3)
            nc.scalar.activation(scaled[0:1, 0, 0:1], ident[0:1, 0:1], ACT.Copy).then_inc(oscale_ok, 1)
            steps(act, body)

        @block.vector
        def _(dve):
            V = nc.vector

            def sort_entries():
                steps_done = [0]

                def link(i):
                    steps_done[0] += 1
                    i.then_inc(sort_step, 1)
                    dve.wait_ge(sort_step, steps_done[0])

                def along(a):
                    return a.unsqueeze(1).broadcast_to([1, NB, NB])

                def across(a):
                    return a.unsqueeze(2).broadcast_to([1, NB, NB])

                dve.wait_ge(number_ok, 1)
                dve.wait_ge(ids_in, 16)
                V.tensor_copy(idf[:], idrow[:])
                link(V.tensor_copy(numberf[:], number[:]))
                link(V.scalar_tensor_tensor(out=key[:], in0=idf[:], scalar=float(NB), in1=numberf[:],
                                            op0=ALU.mult, op1=ALU.add))
                link(V.tensor_tensor(pairs[:, 0], along(key[:]), across(key[:]), ALU.is_lt))
                link(V.tensor_reduce(rank[:], pairs[:, 0], AX.X, ALU.add))
                link(V.tensor_tensor(pairs[:, 0], along(rank[:]), across(numberf[:]), ALU.is_equal))
                V.tensor_tensor(pairs[:, 1], pairs[:, 0], along(numberf[:]), ALU.mult)
                link(V.tensor_tensor(pairs[:, 2], pairs[:, 0], along(idf[:]), ALU.mult))
                link(V.tensor_reduce(sortedf[:], pairs[:, 1:3], AX.X, ALU.add))
                V.tensor_copy(order[:], sortedf[:, 0]).then_inc(order_ok, 1)
                V.tensor_copy(adapter[:], sortedf[:, 1]).then_inc(order_ok, 1)
                V.tensor_tensor(isnew[:, 1:NB], sortedf[:, 1, 1:NB], sortedf[:, 1, 0:NB - 1],
                                ALU.not_equal).then_inc(order_ok, 1)

            sort_entries()
            def split_oscale():
                dve.wait_ge(ocs_in, 16)
                V.tensor_copy(op16[0], ofull).then_inc(opart_ok, 1)
                dve.wait_ge(opart_ok, 1)
                V.tensor_tensor(ofull, ofull, op16[0], ALU.subtract).then_inc(osplit, 1)
                dve.wait_ge(osplit, 1)
                V.tensor_copy(op16[1], ofull).then_inc(opart_ok, 1)
                dve.wait_ge(opart_ok, 2)
                V.tensor_tensor(op16[2], ofull, op16[1], ALU.subtract).then_inc(opart_ok, 1)

            def evac_w(w):
                for half in range(2):
                    dve.wait_ge(wtr_done, 2 * w + half + 1)
                    V.tensor_copy(wt[:, half * HALF:(half + 1) * HALF, w * P:(w + 1) * P], psW[half]).then_inc(wt_ok, 1)

            evac_w(0)
            split_oscale()
            evac_w(1)
            dve.wait_ge(ics_in, 16)
            V.tensor_reduce(absmax[:, NB:NB + 1], icss[:].rearrange("p e c -> p (e c)"), AX.X, ALU.max,
                            apply_absolute_value=True).then_inc(max_ok, 1)
            dve.wait_ge(a_in, 16 * NB)
            V.tensor_copy(acols.rearrange("p c (b r) -> p b c r", b=NB), asel[:]).then_inc(acols_ok, 1)
            V.tensor_reduce(absmax[:, 0:NB], asel[:].rearrange("p b c r -> p b (c r)"), AX.X, ALU.max,
                            apply_absolute_value=True).then_inc(max_ok, 1)
            dve.wait_ge(ident_ok, 4)
            V.tensor_reduce(diag[:], ident[:].rearrange("p (b r) -> p b r", r=R), AX.X, ALU.add).then_inc(prep, 1)
            dve.wait_ge(allmax_ok, 1)
            V.tensor_scalar(allmax[:], allmax[:], 2.0 ** -100, None, ALU.max).then_inc(prep, 1)
            dve.wait_ge(prep, 2)
            V.tensor_scalar(pow2[:].bitcast(I32), allmax[:].bitcast(I32), 0x7F800000, None,
                            ALU.bitwise_and).then_inc(prep, 1)
            dve.wait_ge(prep, 3)
            V.reciprocal(upscale[:], pow2[:]).then_inc(prep, 1)
            V.tensor_scalar(unscale[:], pow2[:, 0:NB], pow2[:, NB:NB + 1], 2.0 ** -13, ALU.mult, ALU.mult).then_inc(prep, 1)
            dve.wait_ge(prep, 4)
            V.tensor_scalar(upscale[:, 0:NB], upscale[:, 0:NB], 2.0 ** 7, None, ALU.mult).then_inc(prep, 1)
            V.tensor_scalar(upscale[:, NB:NB + 1], upscale[:, NB:NB + 1], 2.0 ** 6, None, ALU.mult).then_inc(scale_ok, 1)
            dve.wait_ge(gtiles_done, 1)
            V.tensor_copy(accs[:, 0:P], psA[:, 0:P]).then_inc(gtiles_ok, 1)
            for n in range(Q):
                dve.wait_ge(btr_done, n + 1)
                V.tensor_copy(bc[:, n * CQ:(n + 1) * CQ, :, 0:R],
                              psB[n].rearrange("p (c b r) -> p c b r", c=CQ, b=NB)).then_inc(bt_ok, 1)
                if n == 0:
                    dve.wait_ge(ga_done, 1)
            V.tensor_copy(ga[:], psP[:, 0, 0:E]).then_inc(prep, 1)
            dve.wait_ge(prep, 7)
            V.tensor_tensor(rw[:], ga[:].unsqueeze(1).broadcast_to([P, NB, E]),
                            diag[:].unsqueeze(2).broadcast_to([P, NB, E]), ALU.mult).then_inc(rw_ok, 1)
            evac_w(2)
            for n in range(2):
                dve.wait_ge(bcmm_done, n + 1)
                V.tensor_copy(bc[:, n * HALF:(n + 1) * HALF, :, R:BW],
                              psM[:, n, :].rearrange("p (c b e) -> p c b e", c=HALF, b=NB)).then_inc(bc_ok, 1)

            def g_low(par, grp, count):
                dve.wait_ge(ghigh_ok, count)
                sl = slice(grp * CQ, (grp + 1) * CQ)
                V.tensor_tensor(g[:, par, 1, sl, :], gtmp[:, grp % 2], g[:, par, 0, sl, :], ALU.subtract).then_inc(glow_ok, 1)

            CH = 8

            def softmax(b, n):
                def after(c):
                    dve.wait_ge(chain, b(CH, c))

                logits, bx = acc[:, :, R:BW], acc[:, :, 0:R]

                def parts(i, src):
                    return V.tensor_copy(rparts[:, :, i], src[:].unsqueeze(2).broadcast_to([P, T, PARTS, E]))

                if n == 0:
                    dve.wait_ge(fold_done, b(1, 1))
                    V.tensor_reduce(mx[:], logits, AX.X, ALU.max).then_inc(chain, 1)
                if n == 1:
                    after(1)
                    V.tensor_tensor(ex[:], logits, mx[:].unsqueeze(2).broadcast_to([P, T, E]),
                                    ALU.subtract).then_inc(exp_in, 1)
                if n == 2:
                    dve.wait_ge(exp_ok, b(1, 1))
                    V.tensor_reduce(sm[:], ex[:], AX.X, ALU.add).then_inc(chain, 1)
                if n == 3:
                    after(2)
                    V.reciprocal(rs[:], sm[:]).then_inc(chain, 1)
                if n == 4:
                    after(3)
                    V.tensor_tensor(rt[:], ex[:], rs[:].unsqueeze(2).broadcast_to([P, T, E]),
                                    ALU.mult).then_inc(chain, 1)
                if n == 5:
                    after(4)
                    V.tensor_tensor(pn[:], bx.unsqueeze(3).broadcast_to([P, T, R, E]),
                                    rt[:].unsqueeze(2).broadcast_to([P, T, R, E]), ALU.mult).then_inc(rp_ok, 1)
                if n == 6:
                    parts(0, rt).then_inc(chain, 1)
                if n == 7:
                    after(5)
                    V.tensor_tensor(rd[:], rt[:], rparts[:, :, 0, 0, :], ALU.subtract).then_inc(chain, 1)
                if n == 8:
                    after(6)
                    parts(1, rd).then_inc(chain, 1)
                if n == 9:
                    after(7)
                    V.tensor_tensor(rd[:], rd[:], rparts[:, :, 1, 0, :], ALU.subtract).then_inc(chain, 1)
                if n == 10:
                    after(8)
                    parts(2, rd).then_inc(rp_ok, 1)

            SOFTMAX_OPS = 11

            for w in range(3, WT):
                evac_w(w)
                if 3 <= w < 7 or w >= 8 and w < 12:
                    n = w - 3 if w < 7 else w - 4
                    g_low(n // 4, n % 4, n + 1)
            fixed = lambda per, c: c
            for n in range(SOFTMAX_OPS):
                softmax(fixed, n)

            def body(k, ahead, ahead2):
                nxt = lambda per, c: k.at(per, per + c)

                def add_tile(s):
                    q, t = divmod(s, T)
                    if not ahead and t == POOL_T:
                        return
                    dve.wait_ge(mul_done, k.at(UN, s + 3))
                    dve.wait_ge(xbias_ok, k.at(UN, s + 1))
                    xs = xb[:, k.par, t, q * QW:(q + 1) * QW]
                    V.tensor_tensor(xs, xs, scaled[:, s % OSB], ALU.add).then_inc(out_ok, 1)

                for s in range(UN):
                    q, t = divmod(s, T)
                    first, second = SOFT.get(s, ([], [])) if ahead else ([], [])
                    dve.wait_ge(pre_done, k.at(UN, s + 1))
                    dve.wait_ge(oscale_ok, k.at(UN, s + 2))
                    V.tensor_tensor(scaled[:, s % OSB], psPre[:, s % 2], scaled[:, s % OSB], ALU.mult).then_inc(mul_done, 1)
                    for n in first:
                        softmax(nxt, n)
                    if s >= 1:
                        add_tile(s - 1)
                    if ahead2 and s - 2 in GSLOT:
                        grp = GSLOT[s - 2]
                        g_low(k.par, grp, k.at(Q, 2 * Q + grp + 1))
                    for n in second:
                        softmax(nxt, n)
                add_tile(UN - 1)

            V.memset(mx[:, 0:1], 0.0).then_inc(out_ok, OSB)
            V.memset(mx[:, 1:2], 0.0).then_inc(mul_done, 2)
            steps(dve, body)

        @block.tensor
        def _(pe):
            mm = nc.tensor.matmul

            def transpose_x(u, par, loaded, free):
                if loaded is not None:
                    pe.wait_ge(x_in[par][u // CQ], loaded)
                if free is not None:
                    pe.wait_ge(xT_ok, free)
                for t in range(T):
                    i = nc.tensor.transpose(psT[:, u % 2, t * P:(t + 1) * P], xb[:, par, t, u * P:(u + 1) * P],
                                            ident[:])
                i.then_inc(xtr_done, 1)

            def product_x(grp, par, ready):
                pe.wait_ge(xT_ok, ready)
                for jj in range(CQ):
                    i = mm(psA[jj * CT:(jj + 1) * CT, :], bcur[:, par, grp * CQ + jj, :],
                           xT[:, jj].rearrange("p t n -> p (t n)"), start=(grp == 0), stop=(grp == Q - 1))
                i.then_inc(bx_done, 1)

            def fold_tiles(ready):
                pe.wait_ge(acc_ok, ready)
                for t in range(T):
                    i = mm(acc[:, t, :], accs[:, t * P:(t + 1) * P], fold[:], start=True, stop=True)
                i.then_inc(fold_done, 1)

            def product_m(q, t, par, free, tell=True):
                if t == 0 and free is not None:
                    pe.wait_ge(m_ok, free)
                for c in range(t * CQ, (t + 1) * CQ):
                    for part in range(2):
                        i = mm(psM[:, q % 2, :], g[:, par, part, c, :], wt[:, c, q * QW:(q + 1) * QW],
                               start=(c == 0 and part == 0), stop=(c == C - 1 and part == 1))
                if t == T - 1 and tell:
                    i.then_inc(m_done, 1)

            def transpose_pr(ready, free, psR=psR):
                pe.wait_ge(rp_ok, ready)
                if free is not None:
                    pe.wait_ge(xT_ok, free)
                for t in range(T):
                    nc.tensor.transpose(psP[:, t, :], pn[:, t].rearrange("p r e -> p (r e)"), ident[:])
                for t in range(T):
                    i = nc.tensor.transpose(psR[0:K2, t, :], rparts[:, t].rearrange("p i j e -> p (i j e)"), identb[:])
                i.then_inc(pr_done, 1)

            def transpose_w(w):
                pe.wait_ge(sign_ok, w + 1)
                for half in range(2):
                    if w >= 1:
                        pe.wait_ge(wt_ok, 2 * (w - 1) + half + 1)
                    for c in range(HALF):
                        i = nc.tensor.transpose(psW[half][:, c, :],
                                                sgn[:, w % 2, half * HALF + c:H:C], ident16[:])
                    i.then_inc(wtr_done, 1)

            pe.wait_ge(ident_ok, 4)
            transpose_w(0)
            transpose_w(1)
            pe.wait_ge(gcols_ok, 1)
            pe.wait_ge(acols_ok, 1)
            for c in range(C):
                jj = c % CQ
                i = mm(psA[jj * CT:(jj + 1) * CT, 0:P], bcur[:, 0, c, :], acols[:, c, :], start=(c < CQ), stop=(c >= C - CQ))
            i.then_inc(gtiles_done, 1)
            pe.wait_ge(b_in, 16 * NB)
            for c in range(C):
                i = nc.tensor.transpose(psB[c // CQ][:, (c % CQ) * P:(c % CQ + 1) * P], bsel[:, c * P:(c + 1) * P],
                                        ident[:])
                if c % CQ == CQ - 1:
                    i.then_inc(btr_done, 1)
            pe.wait_ge(gtiles_ok, 1)
            pe.wait_ge(fold_ok, CQ)
            mm(psA[:, 0:E], accs[:, 0:P], fold[:, 0:E], start=True, stop=True).then_inc(ga_done, 1)
            transpose_w(2)
            pe.wait_ge(rw_ok, 1)
            pe.wait_ge(bt_ok, Q)
            for c in range(C):
                i = mm(psM[:, c // HALF, (c % HALF) * NB * E:(c % HALF + 1) * NB * E], bsel[:, c * P:(c + 1) * P],
                       rw[:].rearrange("p b e -> p (b e)"), start=True, stop=True)
                if c % HALF == HALF - 1:
                    i.then_inc(bcmm_done, 1)
            transpose_x(0, 0, 16, None)
            transpose_x(1, 0, None, None)
            for w in range(3, WT + 4):
                if w <= WT:
                    u = w - 1
                    transpose_x(u, 0, 16 if u % CQ == 0 else None, u - 1)
                if w < WT:
                    transpose_w(w)
                if w >= 4:
                    q, t = divmod(w - 4, T)
                    if t == 0:
                        pe.wait_ge(wt_ok, 2 * w)
                        if q == 0:
                            pe.wait_ge(bc_ok, 2)
                    if q == 0:
                        pe.wait_ge(glow_ok, t + 1)
                    product_m(q, t, 0, q - 1 if q >= 2 else None)
                if w <= WT and w % CQ == 0:
                    if w == CQ:
                        pe.wait_ge(bcur_ok, 2)
                        pe.wait_ge(fold_ok, CQ)
                    product_x(w // CQ - 1, 0, w)
                if w == WT + 1:
                    fold_tiles(1)

            def body(k, ahead, ahead2):
                def slots(make_m):
                    for s in range(UN):
                        q, t = divmod(s, T)
                        sl = slice(q * QW, (q + 1) * QW)
                        def transpose(table):
                            u = unit(table, s, ahead, ahead2)
                            if u is None:
                                return
                            if u < C:
                                loaded = k.half(16, 16 + 16 * k.par) if u % CQ == 0 else None
                                transpose_x(u, 1 - k.par, loaded, k.at(C, C + u - 1))
                            else:
                                loaded = k.half(16, 32) if u == C else None
                                transpose_x(u - C, k.par, loaded, k.at(C, C + u - 1))

                        if ahead and s in GROUP:
                            if GROUP[s] == 0:
                                pe.wait_ge(bcur_ok, k.at(2, 4))
                            product_x(GROUP[s], 1 - k.par, k.at(C, C + CQ * (GROUP[s] + 1)))
                        transpose(FIRST)
                        if ahead and s == PTR:
                            transpose_pr(k.at(2, 4), k.at(C, 2 * C + CQ - 1) if ahead2 else None)
                        if make_m and s == UN - 1:
                            product_m(q, t, 1 - k.par, None, False)
                        if s == 0:
                            pe.wait_ge(pT_ok, k.at(1, 1))
                            pe.wait_ge(rT_ok, k.at(1, 1))
                        pe.wait_ge(oscale_ok, k.at(UN, s + 1))
                        mm(psOs[:], rT[:, k.par, t, :], oparts[:, sl], start=True, stop=True).then_inc(os_done, 1)
                        pe.wait_ge(mul_done, k.at(UN, s + 1))
                        mm(psPre[:, s % 2], pT[:, k.par, t, :], m[:, sl], start=True, stop=True).then_inc(pre_done, 1)
                        transpose(SECOND)
                        if make_m and s < UN - 1:
                            if s == 0:
                                pe.wait_ge(glow_ok, k.at(Q, 2 * Q))
                            product_m(q, t, 1 - k.par, None, False)
                        if ahead and s == FOLD:
                            fold_tiles(k.at(1, 2))

                if ahead:
                    k1 = k.at(1, 1)
                    at = isnew[0:1, k1:k1 + 1] if isinstance(k1, int) else isnew[0:1, bass.ds(k1, 1)]
                    new = pe.value_load(at, min_val=0, max_val=1)
                    with pe.If(new == 1):
                        slots(True)
                    with pe.Else():
                        slots(False)
                else:
                    slots(False)

            transpose_pr(2, None, psR0)
            for u in range(CQ):
                transpose_x(u, 1, 16 if u == 0 else None, C + u - 1)
            pe.wait_ge(m_ok, Q)
            pe.wait_ge(order_ok, 3)
            pe.wait_ge(ostack_in, 16 * K2 // E)
            steps(pe, body)


_INS = ['x', 'itok_B_3_7', 'L0_cond_A', 'L0_cond_B', 'L0_ffn_weight', 'L0_ffn_bias', 'L0_ffn_gate_w',
        'L0_ffn_in_channel_scale', 'L0_ffn_out_channel_scale']


def kernel(**inputs):
    import numpy as _np
    import concourse.bacc as _bacc
    from concourse import mybir as _mybir
    from concourse.bass_utils import run_bass_kernel_spmd as _run

    nc = _bacc.Bacc("TRN2", target_bir_lowering=False, num_devices=1, dynamic_dma_scratch_size=1024)
    arrays, args = {}, []
    for name in _INS:
        a = _np.ascontiguousarray(inputs[name])
        arrays[f"in_{name}_dram"] = a
        args.append(nc.dram_tensor(f"in_{name}_dram", a.shape, _mybir.dt.from_np(a.dtype), kind="ExternalInput").ap())
    shape = inputs['x'].shape
    args.append(nc.dram_tensor("out_0_dram", shape, _mybir.dt.float32, kind="ExternalOutput").ap())
    adaln_ffn(nc, *args)
    r = _run(nc, [arrays], core_ids=[0])
    return r.results[0]["out_0_dram"]
```
